# Optimizing a Trainium2 kernel written in Bass

```python
import numpy as np
import jax
import jax.numpy as jnp

def _softmax(x, axis=-1):
    return jax.nn.softmax(x, axis=axis)

def _gelu(x):
    return jax.nn.gelu(x, approximate=True)

def _silu(x):
    return jax.nn.silu(x)

def _sigmoid(x):
    return jax.nn.sigmoid(x)

def _layernorm(x, axis=-1, eps=1e-05):
    m = jnp.mean(x, axis=axis, keepdims=True)
    v = jnp.var(x, axis=axis, keepdims=True)
    return (x - m) / jnp.sqrt(v + eps)

def _scatter_add(tgt, idx, src, axis=0):
    return tgt.at[idx].add(src)

def _segment_sum(src, seg, n):
    return jax.ops.segment_sum(src, seg, n)
kernel_name = 'mk_xattn_seq_d1_seqx_r2_807a65'

def setup_inputs(seed: int=0):
    np.random.seed(seed)
    _w = jnp.asarray

    def _rec_inputs():
        import jax
        import jax.numpy as jnp
        _rk = jax.random.key(seed)
        x = 7.22e-05 + 1 * jax.random.normal(jax.random.fold_in(_rk, 1), (4, 2048, 512), jnp.float32)
        _lenS = 2048 - jax.random.randint(jax.random.fold_in(_rk, 7), (4,), 0, max(1, 2048 // 4) + 1, jnp.int32)
        _lenS2 = 77 - jax.random.randint(jax.random.fold_in(_rk, 8), (4,), 0, max(1, 77 // 4) + 1, jnp.int32)
        _ctx_1024P = jax.random.normal(jax.random.fold_in(_rk, 11), (4, 16, 512), jnp.float32)
        _ctx_1024c = jax.random.dirichlet(jax.random.fold_in(_rk, 511), 0.3 * jnp.ones((16,), jnp.float32), (4, 77))
        _ctx_1024t = jnp.einsum('bsk,bkd->bsd', _ctx_1024c, _ctx_1024P)
        _ctx_1024t = _ctx_1024t * jax.lax.rsqrt(jnp.mean(jnp.square(_ctx_1024t)) + 1e-12) * 0.953939
        ctx_1024 = 4.13588e-05 + 0.999923 * (_ctx_1024t + 0.3 * jax.random.normal(jax.random.fold_in(_rk, 611), (4, 77, 512), jnp.float32))
        _validS = jnp.arange(2048)[None, :] < _lenS[:, None]
        _validS2 = jnp.arange(77)[None, :] < _lenS2[:, None]
        _causal = jnp.tril(jnp.ones((2048, 2048), dtype=bool))
        mask_1x1xSxS2_if1 = jnp.where(jnp.ones((1, 1, 2048, 77), dtype=bool), 1, 0).astype(jnp.int32)
        return (x, ctx_1024, mask_1x1xSxS2_if1)
    x, ctx_1024, mask_1x1xSxS2_if1 = _rec_inputs()

    def _L0_xattn_setup():
        import jax, jax.numpy as jnp
        import numpy as np
        B, S, D, H = (4, 1024, 512, 16)
        DK = D // H

        def _split_heads(x):
            b, s, _ = x.shape
            return x.reshape(b, s, H, DK).transpose(0, 2, 1, 3)
        key = jax.random.key(seed)
        ks = jax.random.split(key, 12)

        def xavier(k, shape):
            fan_in, fan_out = (shape[1], shape[0])
            limit = (6.0 / (fan_in + fan_out)) ** 0.5
            return jax.random.uniform(k, shape, jnp.float32, -limit, limit)
        inp = {'q': jax.random.normal(ks[0], (B, S, D), jnp.float32), 'k': jax.random.normal(ks[1], (B, S, D), jnp.float32), 'v': jax.random.normal(ks[2], (B, S, D), jnp.float32), 'mask': jnp.ones((1, 1, S, S), jnp.int32), 'Wq': xavier(ks[3], (D, D)), 'bq': jnp.zeros((D,), jnp.float32), 'Wk': xavier(ks[4], (D, D)), 'bk': jnp.zeros((D,), jnp.float32), 'Wv': xavier(ks[5], (D, D)), 'bv': jnp.zeros((D,), jnp.float32), 'Wo': xavier(ks[6], (D, D)), 'bo': jnp.zeros((D,), jnp.float32), 'ln_g': jnp.ones((D,), jnp.float32), 'ln_b': jnp.zeros((D,), jnp.float32)}
        return inp
    _L0_xattn_all = _L0_xattn_setup()
    _L0_xattn_in = {k: v for k, v in _L0_xattn_all.items() if k in ('Wq', 'bq', 'Wk', 'bk', 'Wv', 'bv', 'Wo', 'bo', 'ln_g', 'ln_b')}
    del _L0_xattn_all
    return {'x': x, 'ctx_1024': ctx_1024, 'mask_1x1xSxS2_if1': mask_1x1xSxS2_if1, 'L0_xattn_Wq': _L0_xattn_in['Wq'], 'L0_xattn_bq': _L0_xattn_in['bq'], 'L0_xattn_Wk': _L0_xattn_in['Wk'], 'L0_xattn_bk': _L0_xattn_in['bk'], 'L0_xattn_Wv': _L0_xattn_in['Wv'], 'L0_xattn_bv': _L0_xattn_in['bv'], 'L0_xattn_Wo': _L0_xattn_in['Wo'], 'L0_xattn_bo': _L0_xattn_in['bo'], 'L0_xattn_ln_g': _L0_xattn_in['ln_g'], 'L0_xattn_ln_b': _L0_xattn_in['ln_b']}

def reference(x, ctx_1024, mask_1x1xSxS2_if1, L0_xattn_Wq, L0_xattn_bq, L0_xattn_Wk, L0_xattn_bk, L0_xattn_Wv, L0_xattn_bv, L0_xattn_Wo, L0_xattn_bo, L0_xattn_ln_g, L0_xattn_ln_b):
    import jax
    import jax.numpy as jnp

    def _L0_xattn_ref(q, k, v, mask, Wq, bq, Wk, bk, Wv, bv, Wo, bo, ln_g, ln_b):
        import jax, jax.numpy as jnp
        import numpy as np
        B, S, D, H = (4, 1024, 512, 16)
        DK = D // H

        def _split_heads(x):
            b, s, _ = x.shape
            return x.reshape(b, s, H, DK).transpose(0, 2, 1, 3)
        residual = q
        qh = _split_heads(q @ Wq.T + bq)
        kh = _split_heads(k @ Wk.T + bk)
        vh = _split_heads(v @ Wv.T + bv)
        scale = jnp.sqrt(jnp.asarray(DK, qh.dtype))
        scores = jnp.einsum('bhqd,bhkd->bhqk', qh, kh) / scale
        scores = jnp.where(mask == 0, jnp.asarray(-1000000000.0, scores.dtype), scores)
        m = jnp.max(scores, axis=-1, keepdims=True)
        e = jnp.exp(scores - m) * mask.astype(scores.dtype)
        probs = e / (jnp.sum(e, axis=-1, keepdims=True) + 1e-09)
        attn = jnp.einsum('bhqk,bhkd->bhqd', probs, vh)
        attn = attn.transpose(0, 2, 1, 3).reshape(q.shape[0], -1, D)
        out = attn @ Wo.T + bo
        x = out + residual
        mu = jnp.mean(x, axis=-1, keepdims=True)
        var = jnp.mean((x - mu) ** 2, axis=-1, keepdims=True)
        return (x - mu) / jnp.sqrt(var + 1e-05) * ln_g + ln_b
    x = _L0_xattn_ref(x, ctx_1024, ctx_1024, mask_1x1xSxS2_if1, L0_xattn_Wq, L0_xattn_bq, L0_xattn_Wk, L0_xattn_bk, L0_xattn_Wv, L0_xattn_bv, L0_xattn_Wo, L0_xattn_bo, L0_xattn_ln_g, L0_xattn_ln_b)
    return x

_drawn_inputs = setup_inputs


def setup_inputs(seed=0):
    import zlib

    import numpy as np

    out = dict(_drawn_inputs(seed))
    spreads = {'L0_xattn_bq': (0.0, 0.385),
     'L0_xattn_bk': (0.0, 0.8),
     'L0_xattn_bv': (0.0, 0.1),
     'L0_xattn_bo': (0.0, 0.1),
     'L0_xattn_ln_g': (1.0, 0.2),
     'L0_xattn_ln_b': (0.0, 0.1)}
    factors = {}
    for name, (base, spread) in spreads.items():
        noise = np.random.default_rng([zlib.crc32(name.encode()), seed]).standard_normal(out[name].shape)
        drawn = base * np.exp(spread * noise) if base else spread * noise
        out[name] = jnp.asarray(drawn.astype(out[name].dtype))
    for name, factor in factors.items():
        out[name] = (out[name] * factor).astype(out[name].dtype)
    return out
```

```python
from contextlib import ExitStack

import numpy as np

import concourse.bass as bass
from concourse import mybir

FP32 = mybir.dt.float32
FP32R = mybir.dt.float32r
BF16 = mybir.dt.bfloat16
I32 = mybir.dt.int32
ALU = mybir.AluOpType
ACT = mybir.ActivationFunctionType
AX = mybir.AxisListType


def xattn_program(nc, x, ctx, mask, Wq, bq, Wk, bk, Wv, bv, Wo, bo, ln_g, ln_b, out):
    B, S, D = x.shape
    SK = ctx.shape[1]
    H = 16
    DK = D // H
    P = 128
    C = D // P
    HG = H // C
    GK = HG * SK
    T = 4
    ROWS = T * P
    NB = B * S // ROWS
    NT = NB * T
    BB = S // ROWS
    MT = S // P
    RING = 3
    SCALE = float(np.sqrt(np.float32(DK)))
    NEG = -1e9 * SCALE
    LN_EPS = 1e-5
    SUM_EPS = 1e-9
    STEPS = NB + 3
    LOOP_FROM, LOOP_TO = 3, 3 + (NB - 3) // 2 * 2

    x_rows = x.rearrange("b s d -> (b s) d").rearrange("(n p) d -> n p d", p=P)
    out_rows = out.rearrange("b s d -> (b s) d").rearrange("(n p) d -> n p d", p=P)

    es = ExitStack()
    with es:
        def sb(name, shape, dt):
            return es.enter_context(nc.sbuf_tensor(name, shape, dt))

        def sem(name):
            return es.enter_context(nc.semaphore(name))

        ident = sb("ident", [P, P], FP32)
        minus_half = sb("minus_half", [P, 1], FP32)
        ln_eps = sb("ln_eps", [P, 1], FP32)
        WqT_hi = sb("WqT_hi", [P, C, D], FP32R)
        WqT_lo = sb("WqT_lo", [P, C, D], FP32R)
        WoT_hi = sb("WoT_hi", [P, C, D], FP32R)
        WoT_lo = sb("WoT_lo", [P, C, D], FP32R)
        K_diag = sb("K_diag", [P, B, C, HG, SK], FP32)
        V_all = sb("V_all", [SK, B, D], FP32)
        V_now = sb("V_now", [SK, D], FP32)
        mask_f = sb("mask_f", [P, MT, SK], FP32)
        mask_bias = sb("mask_bias", [P, MT, SK], BF16)
        qk_bias = sb("qk_bias", [P, 2 * C], FP32)
        bo_row = sb("bo_row", [P, D], FP32)
        g_row = sb("g_row", [P, D], FP32)
        b_row = sb("b_row", [P, D], FP32)

        x_in = sb("x_in", [P, T, D], FP32)
        x_bo = sb("x_bo", [P, RING, T, D], FP32)
        xT_hi = sb("xT_hi", [P, C, ROWS], FP32R)
        xT_lo = sb("xT_lo", [P, C, ROWS], FP32R)
        QT = sb("QT", [P, 2, C, ROWS], FP32)
        E = sb("E", [P, T, H, SK], FP32)
        PT = sb("PT", [P, H, ROWS], FP32)
        AT_hi = sb("AT_hi", [P, C, ROWS], FP32R)
        AT_lo = sb("AT_lo", [P, C, ROWS], FP32R)
        Y = sb("Y", [P, T, D], FP32)
        rowmax = sb("rowmax", [P, T, H], FP32)
        rowsum = sb("rowsum", [P, T, H], FP32)
        rowsum_eps = sb("rowsum_eps", [P, T, H], FP32)
        inv_sum = sb("inv_sum", [P, T, H], FP32)
        bn = sb("bn", [P, T, 6], FP32)
        mean_var = sb("mean_var", [P, T, 2], FP32)
        var_eps = sb("var_eps", [P, T], FP32)
        rstd = sb("rstd", [P, T], FP32)

        W_nat = {n: PT[:, C * i:C * i + C, :] for i, n in enumerate("kvqo")}
        flat = E[:, :, :, :].rearrange("p t h k -> p (t h k)")
        ctx_nat = flat[0:SK, 0:B * D].rearrange("p (b d) -> p b d", b=B)
        ctxT = flat[:, B * D:B * D + C * B * SK].rearrange("p (c b k) -> p c b k", c=C, b=B)
        bv_at = B * D + C * B * SK
        bv_row = flat[0:SK, bv_at:bv_at + D]
        qk_nat = flat[0:2 * C, bv_at + D:bv_at + D + P]
        WkT = QT[:, 0, :, :]
        WvT = QT[:, 1, :, :]
        mask_i = Y[:, :, :].rearrange("p t d -> p (t d)")[:, 0:MT * SK].bitcast(I32) \
            .rearrange("p (t k) -> p t k", t=MT)

        banks = [es.enter_context(nc.psum_tensor(f"bank{i}", [P, 4, 512], FP32)) if i == 0 else
                 es.enter_context(nc.psum_tensor(f"bank{i}", [P, 512], FP32)) for i in (0, 4, 5, 6, 7)]
        scores_ps, xq_ps, pt_ps_bank, av_bank, out_bank = banks
        vo_banks = [av_bank, out_bank]

        def prep_bank(n):
            return scores_ps[:, n % 6, :] if n % 6 < 4 else vo_banks[n % 6 - 4][:, :]

        w_loaded = {n: sem(f"w{n}_loaded") for n in "kvqo"}
        ctx_loaded = sem("ctx_loaded")
        qk_loaded = sem("qk_loaded")
        bv_loaded = sem("bv_loaded")
        rows_loaded = sem("rows_loaded")
        mask_loaded = sem("mask_loaded")
        ident_zeroed = sem("ident_zeroed")
        ident_ready = sem("ident_ready")
        K_zeroed = sem("K_zeroed")
        prep_ps = sem("prep_ps")
        prep_act = sem("prep_act")
        prep_dve = sem("prep_dve")
        mask_ready = sem("mask_ready")
        x_loaded = [sem(f"x_loaded{i}") for i in range(T)]
        xt_ps = sem("xt_ps")
        xt_hi = sem("xt_hi")
        xt_lo = sem("xt_lo")
        x_bo_ready = sem("x_bo_ready")
        q_ps = sem("q_ps")
        q_ready = sem("q_ready")
        s_ps = sem("s_ps")
        biased = sem("biased")
        max_ready = sem("max_ready")
        shifted = sem("shifted")
        exp_ready = sem("exp_ready")
        weighted = sem("weighted")
        sum_ready = sem("sum_ready")
        sum_eps_ready = sem("sum_eps_ready")
        inv_ready = sem("inv_ready")
        probs_ready = sem("probs_ready")
        pt_ps = sem("pt_ps")
        pt_ready = sem("pt_ready")
        v_ready = sem("v_ready")
        av_ps = sem("av_ps")
        at_hi = sem("at_hi")
        at_lo = sem("at_lo")
        out_ps = sem("out_ps")
        y_ready = sem("y_ready")
        bn_ready = sem("bn_ready")
        aggr_turn = sem("aggr_turn")
        stats_ready = sem("stats_ready")
        centered = sem("centered")
        var_eps_ready = sem("var_eps_ready")
        rstd_ready = sem("rstd_ready")
        scaled = sem("scaled")
        normed = sem("normed")
        stored = [sem(f"stored{i}") for i in range(T)]

        block = es.enter_context(nc.Block())

        PREP = ([("bias", None, 0)] + [("wT", "q", c) for c in range(C)] + [("wT", "k", c) for c in range(C)] +
                [("ctxT", None, c) for c in range(C)] + [("K", None, g) for g in range(C)] +
                [("wT", "v", c) for c in range(C)] + [("V", None, b) for b in range(B)] +
                [("wT", "o", c) for c in range(C)])
        FILLS_BEFORE = 1 + C
        FILLS_EACH = (len(PREP) - FILLS_BEFORE) // (2 * T)

        def fills_behind(unit):
            at = FILLS_BEFORE + unit * FILLS_EACH
            return range(at, at + FILLS_EACH)

        def readers(use):
            kind, w, _ = use
            if kind == "wT" and w in "qo":
                return ("act", "dve")
            return ("act",) if (kind, w) in (("wT", "k"), ("K", None)) else ("dve",)

        def prep_count(engine, n):
            return sum(engine in readers(u) for u in PREP[:n])

        def position(kind, w=None):
            return max(n for n, u in enumerate(PREP) if u[:2] == (kind, w)) + 1

        def valid(tile):
            return not isinstance(tile, int) or 0 <= tile < NT

        def has(b):
            return not isinstance(b, int) or 0 <= b < NB

        def steps(engine, step):
            for s in range(1, LOOP_FROM):
                step(s, s % 2)
            with engine.Fori(0, (LOOP_TO - LOOP_FROM) // 2) as i:
                step(2 * i + LOOP_FROM, LOOP_FROM % 2)
                step(2 * i + LOOP_FROM + 1, (LOOP_FROM + 1) % 2)
            for s in range(LOOP_TO, STEPS):
                step(s, s % 2)

        @block.sync
        def _(sp):
            def load_w(n, w):
                sp.dma_start(W_nat[n], w.rearrange("(i p) d -> p i d", p=P)).then_inc(w_loaded[n], 16)

            load_w("q", Wq)
            for i in range(T):
                sp.dma_start(x_in[:, i, :], x_rows[i]).then_inc(x_loaded[i], 16)
            load_w("k", Wk)
            sp.dma_start(ctx_nat, ctx.rearrange("b k d -> k b d")).then_inc(ctx_loaded, 16)
            load_w("v", Wv)
            load_w("o", Wo)

            def step(s, parity):
                b_out = s - 3
                b_next = s + 1
                for i in range(T):
                    if has(b_out):
                        sp.wait_ge(normed, 4 * b_out + i + 1)
                        sp.dma_start(out_rows[bass.ds(4 * b_out + i, 1)].rearrange("a p d -> p (a d)"),
                                     Y[:, i, :]).then_inc(stored[i], 16)
                    if i == 1 and has(s) and has(b_next):
                        for n in range(T):
                            sp.wait_ge(xt_ps, 4 * s + n + 1)
                            sp.wait_ge(x_bo_ready, 4 * s + n + 1)
                            sp.dma_start(x_in[:, n, :],
                                         x_rows[bass.ds(4 * b_next + n, 1)].rearrange("a p d -> p (a d)")) \
                                .then_inc(x_loaded[n], 16)

            step(0, 0)
            steps(sp, step)
            for i in range(T):
                sp.wait_ge(stored[i], 16 * NB)

        @block.tensor
        def _(pe):
            mm = nc.tensor.matmul

            def fill(n):
                kind, w, c = PREP[n]
                bank = prep_bank(n)
                if n >= 6:
                    pe.wait_ge(prep_act, prep_count("act", n - 5))
                    pe.wait_ge(prep_dve, prep_count("dve", n - 5))
                if kind == "bias":
                    pe.wait_ge(qk_loaded, 32)
                    last = nc.tensor.transpose(bank[:, 0:2 * C], qk_nat, ident[0:2 * C, 0:2 * C])
                elif kind == "wT":
                    if c == 0:
                        pe.wait_ge(w_loaded[w], 16)
                    for i in range(C):
                        last = nc.tensor.transpose(bank[:, i * P:i * P + P], W_nat[w][:, i, c * P:c * P + P],
                                                   ident[:, :])
                elif kind == "ctxT":
                    if c == 0:
                        pe.wait_ge(ctx_loaded, 16)
                    for b in range(B):
                        last = nc.tensor.transpose(bank[:, b * SK:b * SK + SK],
                                                   ctx_nat[:, b, c * P:c * P + P], ident[0:SK, 0:SK])
                elif kind == "K":
                    pe.wait_ge(prep_act, prep_count("act", position("wT", "k")))
                    pe.wait_ge(prep_dve, prep_count("dve", position("ctxT")))
                    for k in range(C):
                        last = mm(bank[:, 0:B * SK], WkT[:, k, c * P:c * P + P],
                                  ctxT[:, k, :, :].rearrange("p b k -> p (b k)"),
                                  start=(k == 0), stop=(k == C - 1))
                else:
                    pe.wait_ge(prep_dve, prep_count("dve", position("wT", "v")))
                    for k in range(C):
                        last = mm(bank[0:SK, :], ctxT[:, k, c, :], WvT[:, k, :],
                                  start=(k == 0), stop=(k == C - 1))
                last.then_inc(prep_ps, 1)

            def step(s, parity):
                bx, bs, ba, bo_ = s, s - 1, s - 2, s - 3

                def XT(i):
                    if not has(bx):
                        return
                    pe.wait_ge(x_loaded[i], 16 * bx + 16)
                    if i:
                        pe.wait_ge(xt_lo, 4 * bx + i)
                    elif not isinstance(bx, int) or bx:
                        pe.wait_ge(q_ready, 4 * bx)
                    for k in range(C):
                        last = nc.tensor.transpose(xq_ps[:, k * P:k * P + P], x_in[:, i, k * P:k * P + P],
                                                   ident[:, :])
                    last.then_inc(xt_ps, 1)

                def Q(g):
                    if not has(bx):
                        return
                    if g:
                        pe.wait_ge(q_ready, 4 * bx + g)
                    else:
                        pe.wait_ge(xt_lo, 4 * bx + 4)
                    if isinstance(bx, int) and bx == 0:
                        pe.wait_ge(prep_dve, prep_count("dve", position("wT", "q")))
                    n = 0
                    for w, r in ((WqT_lo, xT_hi), (WqT_hi, xT_lo), (WqT_hi, xT_hi)):
                        for k in range(C):
                            last = mm(xq_ps[:, :], w[:, k, g * P:g * P + P], r[:, k, :],
                                      start=(n == 0), stop=(n == 3 * C - 1))
                            n += 1
                    last.then_inc(q_ps, 1)

                def S(t, half):
                    if not has(bs):
                        return
                    tile = 4 * bs + t
                    if t == 0 and half == 0:
                        pe.wait_ge(q_ready, 4 * bs + 4)
                    if not isinstance(tile, int) or tile:
                        pe.wait_ge(biased, 2 * tile - 1 + half)
                    batch = bs // BB
                    for g in (2 * half, 2 * half + 1):
                        last = mm(scores_ps[:, g, 0:GK], QT[:, 1 - parity, g, t * P:t * P + P],
                                  K_diag[:, bass.ds(batch, 1), g, :, :].rearrange("p b j k -> p (b j k)"),
                                  start=True, stop=True)
                    last.then_inc(s_ps, 1)

                def PTr(t, g):
                    tile = 4 * bs + t - 3
                    if not valid(tile):
                        return
                    if g == 0:
                        pe.wait_ge(probs_ready, tile + 1)
                    if not isinstance(tile, int) or 4 * tile + g:
                        pe.wait_ge(pt_ready, 4 * tile + g)
                    for j in range(HG):
                        last = nc.tensor.transpose(pt_ps_bank[0:SK, j * P:j * P + P],
                                                   E[:, (t + 1) % 4, HG * g + j, :], ident[:, :])
                    last.then_inc(pt_ps, 1)

                def AV(g):
                    if not has(ba):
                        return
                    if g == 0:
                        pe.wait_ge(pt_ready, 16 * ba + 16)
                        pe.wait_ge(v_ready, ba + 1)
                    if g >= 2:
                        pe.wait_ge(at_lo, 4 * ba + g - 1)
                    elif not isinstance(ba, int) or ba:
                        pe.wait_ge(y_ready, 4 * ba - 1 + g)
                    for j in range(HG):
                        h = HG * g + j
                        last = mm(vo_banks[g % 2][DK * j:DK * j + DK, :], V_now[:, DK * h:DK * h + DK],
                                  PT[0:SK, h, :], start=True, stop=True, tile_position=(0, DK * j))
                    last.then_inc(av_ps, 1)

                def OUT(i):
                    if not has(bo_):
                        return
                    if i == 0:
                        pe.wait_ge(at_lo, 4 * bo_ + 4)
                    if i >= 2:
                        pe.wait_ge(y_ready, 4 * bo_ + i - 1)
                    n = 0
                    for a, w in ((AT_hi, WoT_lo), (AT_lo, WoT_hi), (AT_hi, WoT_hi)):
                        for k in range(C):
                            last = mm(vo_banks[i % 2][:, :], a[:, k, i * P:i * P + P], w[:, k, :],
                                      start=(n == 0), stop=(n == 3 * C - 1))
                            n += 1
                    last.then_inc(out_ps, 1)

                if isinstance(s, int) and s == 0:
                    for unit in range(2 * T):
                        XT(unit) if unit < T else Q(unit - T)
                        for n in fills_behind(unit):
                            fill(n)
                    pe.wait_ge(prep_act, prep_count("act", len(PREP)))
                    pe.wait_ge(prep_dve, prep_count("dve", len(PREP)))
                    return
                S(0, 0), PTr(0, 0), XT(0), OUT(0), PTr(0, 1), XT(1), S(0, 1), PTr(0, 2), XT(2), OUT(1)
                PTr(0, 3), XT(3)
                S(1, 0), PTr(1, 0), Q(0), PTr(1, 1), S(1, 1), PTr(1, 2), OUT(2), PTr(1, 3)
                S(2, 0), PTr(2, 0), Q(1), PTr(2, 1), S(2, 1), OUT(3), PTr(2, 2), Q(2), PTr(2, 3)
                S(3, 0), Q(3), AV(0), AV(1), PTr(3, 0), AV(2), PTr(3, 1), S(3, 1), AV(3), PTr(3, 2), PTr(3, 3)

            pe.wait_ge(ident_ready, 1)
            for n in range(FILLS_BEFORE):
                fill(n)
            step(0, 0)
            steps(pe, step)

        @block.scalar
        def _(act):
            cp = nc.scalar.activation
            act.dma_start(qk_nat[0:C, :], bq.rearrange("(g p) -> g p", p=P)).then_inc(qk_loaded, 16)
            act.dma_start(qk_nat[C:2 * C, :], bk.rearrange("(g p) -> g p", p=P)).then_inc(qk_loaded, 16)
            act.dma_start(mask_i, mask.rearrange("a b (t p) k -> p (a b t) k", p=P)).then_inc(mask_loaded, 16)
            act.dma_start(bv_row, bv.rearrange("(a n) -> a n", a=1).broadcast_to((SK, D))).then_inc(bv_loaded, 16)
            for row, vector in ((bo_row, bo), (g_row, ln_g), (b_row, ln_b)):
                act.dma_start(row[:, :], vector.rearrange("(a n) -> a n", a=1).broadcast_to((P, D))) \
                    .then_inc(rows_loaded, 16)

            def fill_out(n):
                kind, w, c = PREP[n]
                if "act" not in readers(PREP[n]):
                    return
                bank = prep_bank(n)
                act.wait_ge(prep_ps, n + 1)
                if kind == "K":
                    act.wait_ge(K_zeroed, 1)
                    act.wait_ge(prep_dve, 1)
                    for j in range(HG):
                        rows = slice(DK * j, DK * j + DK)
                        last = cp(K_diag[rows, :, c, j, :],
                                  bank[rows, 0:B * SK].rearrange("p (b k) -> p b k", b=B),
                                  ACT.Identity, bias=qk_bias[rows, C + c:C + c + 1])
                else:
                    last = cp({"k": WkT, "q": WqT_hi, "o": WoT_hi}[w][:, c, :], bank, ACT.Copy)
                last.then_inc(prep_act, 1)

            def step(s, parity):
                bx, bs, ba, bo_ = s, s - 1, s - 2, s - 3

                def XT_hi(i):
                    if not has(bx):
                        return
                    act.wait_ge(xt_ps, 4 * bx + i + 1)
                    cp(xT_hi[:, :, i * P:i * P + P], xq_ps[:, :].rearrange("p (k r) -> p k r", k=C),
                       ACT.Copy).then_inc(xt_hi, 1)

                def Q_out(g):
                    if not has(bx):
                        return
                    act.wait_ge(q_ps, 4 * bx + g + 1)
                    cp(QT[:, parity, g, :], xq_ps[:, :], ACT.Identity, bias=qk_bias[:, g:g + 1]) \
                        .then_inc(q_ready, 1)

                def exponent(t):
                    tile = 4 * bs + t - 1
                    if not valid(tile):
                        return
                    act.wait_ge(shifted, tile + 1)
                    e = E[:, (t + 3) % 4, :, :]
                    cp(e, e, ACT.Exp, scale=1.0 / SCALE).then_inc(exp_ready, 1)

                def PT_out(t, g):
                    tile = 4 * bs + t - 3
                    if not valid(tile):
                        return
                    act.wait_ge(pt_ps, 4 * tile + g + 1)
                    i = (t + 1) % 4
                    cp(PT[0:SK, HG * g:HG * g + HG, i * P:i * P + P],
                       pt_ps_bank[0:SK, :].rearrange("p (j r) -> p j r", j=HG), ACT.Copy).then_inc(pt_ready, 1)

                def V_copy():
                    if not has(ba):
                        return
                    if not isinstance(ba, int) or ba:
                        act.wait_ge(av_ps, 4 * ba)
                    cp(V_now[:, :], V_all[:, bass.ds(ba // BB, 1), :].rearrange("p b d -> p (b d)"),
                       ACT.Copy).then_inc(v_ready, 1)

                def AV_hi(g):
                    if not has(ba):
                        return
                    act.wait_ge(av_ps, 4 * ba + g + 1)
                    cp(AT_hi[:, g, :], vo_banks[g % 2][:, :], ACT.Copy).then_inc(at_hi, 1)

                def LN_scale(i):
                    if not has(bo_):
                        return
                    act.wait_ge(centered, 4 * bo_ + i + 1)
                    act.wait_ge(rstd_ready, 4 * bo_ + i + 1)
                    cp(Y[:, i, :], Y[:, i, :], ACT.Copy, scale=rstd[:, i:i + 1]).then_inc(scaled, 1)

                if isinstance(s, int) and s == 0:
                    act.wait_ge(prep_dve, 1)
                    for unit in range(2 * T):
                        XT_hi(unit) if unit < T else Q_out(unit - T)
                        for n in fills_behind(unit):
                            fill_out(n)
                    return
                PT_out(0, 0), XT_hi(0), PT_out(0, 1), XT_hi(1), PT_out(0, 2), XT_hi(2), exponent(0)
                PT_out(0, 3), XT_hi(3)
                PT_out(1, 0), Q_out(0), PT_out(1, 1), exponent(1), PT_out(1, 2), LN_scale(0), PT_out(1, 3), LN_scale(1)
                PT_out(2, 0), Q_out(1), PT_out(2, 1), exponent(2), PT_out(2, 2), V_copy(), Q_out(2), LN_scale(2)
                PT_out(2, 3)
                Q_out(3), AV_hi(0), AV_hi(1), PT_out(3, 0), AV_hi(2), PT_out(3, 1), exponent(3), AV_hi(3)
                PT_out(3, 2), LN_scale(3), PT_out(3, 3)

            for n in range(FILLS_BEFORE):
                fill_out(n)
            step(0, 0)
            steps(act, step)

        @block.vector
        def _(dve):
            tt = nc.vector.tensor_tensor

            nc.vector.memset(K_diag[:, :, :, :, :], 0.0).then_inc(K_zeroed, 1)

            def fill_out(n):
                kind, w, c = PREP[n]
                if "dve" not in readers(PREP[n]):
                    return
                bank = prep_bank(n)
                dve.wait_ge(prep_ps, n + 1)
                if kind == "bias":
                    last = nc.vector.tensor_copy(qk_bias[:, :], bank[:, 0:2 * C])
                elif kind == "ctxT":
                    last = nc.vector.tensor_copy(ctxT[:, c, :, :],
                                                 bank[:, 0:B * SK].rearrange("p (b k) -> p b k", b=B))
                elif kind == "V":
                    dve.wait_ge(bv_loaded, 16)
                    last = tt(V_all[:, c, :], bank[0:SK, :], bv_row, ALU.add)
                elif w == "v":
                    last = nc.vector.tensor_copy(WvT[:, c, :], bank)
                else:
                    hi, lo = {"q": (WqT_hi, WqT_lo), "o": (WoT_hi, WoT_lo)}[w]
                    dve.wait_ge(prep_act, prep_count("act", n + 1))
                    last = tt(lo[:, c, :], bank, hi[:, c, :].bitcast(FP32), ALU.subtract)
                last.then_inc(prep_dve, 1)

            def masks():
                dve.wait_ge(mask_loaded, 16)
                nc.vector.tensor_copy(mask_f[:, :, :], mask_i).then_inc(mask_ready, 1)
                dve.wait_ge(mask_ready, 1)
                nc.vector.tensor_scalar(mask_bias[:, :, :], mask_f[:, :, :], 0.0, NEG,
                                        ALU.is_equal, ALU.mult).then_inc(mask_ready, 1)

            def step(s, parity):
                bx, bs, ba, bo_ = s, s - 1, s - 2, s - 3

                def XT_lo(i):
                    if not has(bx):
                        return
                    dve.wait_ge(xt_hi, 4 * bx + i + 1)
                    cols = slice(i * P, i * P + P)
                    tt(xT_lo[:, :, cols], xq_ps[:, :].rearrange("p (k r) -> p k r", k=C),
                       xT_hi[:, :, cols].bitcast(FP32), ALU.subtract).then_inc(xt_lo, 1)

                def bias(t, half):
                    tile = 4 * bs + t
                    if not valid(tile):
                        return
                    dve.wait_ge(s_ps, 2 * tile + half + 1)
                    if half == 0 and (not isinstance(tile, int) or tile >= 4):
                        dve.wait_ge(pt_ps, 4 * tile - 12)
                    tt(E[:, t, 2 * HG * half:2 * HG * half + 2 * HG, :].rearrange("p (g j) k -> p g j k", g=2),
                       scores_ps[:, 2 * half:2 * half + 2, 0:GK].rearrange("p g (j k) -> p g j k", j=HG),
                       mask_bias[:, bass.ds(bs % BB * T + t, 1), :].unsqueeze(2).broadcast_to((P, 2, HG, SK)),
                       ALU.add).then_inc(biased, 1)

                def row_max(t):
                    tile = 4 * bs + t
                    if not valid(tile):
                        return
                    dve.wait_ge(biased, 2 * tile + 2)
                    nc.vector.tensor_reduce(out=rowmax[:, t, :], in_=E[:, t, :, :], op=ALU.max, axis=AX.X) \
                        .then_inc(max_ready, 1)

                def shift(t):
                    tile = 4 * bs + t
                    if not valid(tile):
                        return
                    dve.wait_ge(max_ready, tile + 1)
                    e = E[:, t, :, :]
                    tt(e, e, rowmax[:, t, :].unsqueeze(2).broadcast_to((P, H, SK)), ALU.subtract) \
                        .then_inc(shifted, 1)

                def row_sum(t):
                    tile = 4 * bs + t - 2
                    if not valid(tile):
                        return
                    i = (t + 2) % 4
                    dve.wait_ge(weighted, tile + 1)
                    nc.vector.tensor_reduce(out=rowsum[:, i, :], in_=E[:, i, :, :], op=ALU.add, axis=AX.X) \
                        .then_inc(sum_ready, 1)

                def sum_eps(t):
                    tile = 4 * bs + t - 2
                    if not valid(tile):
                        return
                    i = (t + 2) % 4
                    dve.wait_ge(sum_ready, tile + 1)
                    nc.vector.tensor_scalar(rowsum_eps[:, i, :], rowsum[:, i, :], SUM_EPS, None, ALU.add) \
                        .then_inc(sum_eps_ready, 1)

                def inverse(t):
                    tile = 4 * bs + t - 2
                    if not valid(tile):
                        return
                    i = (t + 2) % 4
                    dve.wait_ge(sum_eps_ready, tile + 1)
                    nc.vector.reciprocal(inv_sum[:, i, :], rowsum_eps[:, i, :]).then_inc(inv_ready, 1)

                def AV_lo(g):
                    if not has(ba):
                        return
                    dve.wait_ge(at_hi, 4 * ba + g + 1)
                    tt(AT_lo[:, g, :], vo_banks[g % 2][:, :], AT_hi[:, g, :].bitcast(FP32), ALU.subtract) \
                        .then_inc(at_lo, 1)

                def residual(i):
                    if not has(bo_):
                        return
                    tile = 4 * bo_ + i
                    dve.wait_ge(out_ps, tile + 1)
                    dve.wait_ge(x_bo_ready, tile + 1)
                    if not isinstance(bo_, int) or bo_:
                        dve.wait_ge(stored[i], 16 * bo_)
                    tt(Y[:, i, :], vo_banks[i % 2][:, :],
                       x_bo[:, bass.ds(bo_ % RING, 1), i, :].rearrange("p r d -> p (r d)"), ALU.add) \
                        .then_inc(y_ready, 1)

                def stats(i):
                    if not has(bo_):
                        return
                    dve.wait_ge(y_ready, 4 * bo_ + i + 1)
                    nc.vector.bn_stats(bn[:, i, :], Y[:, i, :]).then_inc(bn_ready, 1)

                def aggregate(i):
                    if not has(bo_):
                        return
                    dve.wait_ge(bn_ready, 4 * bo_ + i + 1)
                    dve.sem_inc(aggr_turn, 1)
                    nc.vector.bn_aggr(mean_var[:, i, :], bn[:, i, :]).then_inc(stats_ready, 1)

                def center(i):
                    if not has(bo_):
                        return
                    dve.wait_ge(stats_ready, 4 * bo_ + i + 1)
                    nc.vector.scalar_tensor_tensor(out=Y[:, i, :], in0=Y[:, i, :], scalar=mean_var[:, i, 0:1],
                                                   in1=g_row[:, :], op0=ALU.subtract, op1=ALU.mult) \
                        .then_inc(centered, 1)

                if isinstance(s, int) and s == 0:
                    for unit in range(2 * T):
                        if unit < T:
                            XT_lo(unit)
                        if unit == T:
                            masks()
                        for n in fills_behind(unit):
                            fill_out(n)
                    dve.wait_ge(mask_ready, 2)
                    dve.wait_ge(rows_loaded, 48)
                    return
                row_sum(0), bias(0, 0), sum_eps(0), XT_lo(0), inverse(0), residual(0), XT_lo(1), stats(0), bias(0, 1)
                aggregate(0), XT_lo(2), row_max(0), residual(1), XT_lo(3), shift(0)
                row_sum(1), bias(1, 0), sum_eps(1), stats(1), inverse(1), center(0), aggregate(1), bias(1, 1)
                residual(2), center(1), row_max(1), stats(2), shift(1), aggregate(2)
                row_sum(2), bias(2, 0), sum_eps(2), center(2), inverse(2), bias(2, 1), row_max(2), residual(3), shift(2)
                stats(3)
                row_sum(3), aggregate(3), bias(3, 0), sum_eps(3), center(3), inverse(3), AV_lo(0), AV_lo(1), AV_lo(2)
                bias(3, 1), AV_lo(3), row_max(3), shift(3)

            for n in range(FILLS_BEFORE):
                fill_out(n)
            step(0, 0)
            steps(dve, step)

        @block.gpsimd
        def _(pool):
            nc.gpsimd.memset(ident[:, :], 0.0).then_inc(ident_zeroed, 1)
            nc.gpsimd.memset(minus_half[:, :], -0.5).then_inc(ident_zeroed, 1)
            nc.gpsimd.memset(ln_eps[:, :], LN_EPS).then_inc(ident_zeroed, 1)
            pool.wait_ge(ident_zeroed, 3)
            nc.gpsimd.affine_select(out=ident[:, :], in_=ident[:, :], compare_op=ALU.not_equal, fill=1.0,
                                    base=0, pattern=[[-1, P]], channel_multiplier=1).then_inc(ident_ready, 1)
            pool.wait_ge(rows_loaded, 48)

            def step(s, parity):
                bx, bs, bo_ = s, s - 1, s - 3

                def add_bo(i):
                    if not has(bx):
                        return
                    pool.wait_ge(x_loaded[i], 16 * bx + 16)
                    if not isinstance(bx, int) or bx >= RING:
                        pool.wait_ge(y_ready, 4 * (bx - RING) + i + 1)
                    nc.gpsimd.tensor_tensor(out=x_bo[:, bass.ds(bx % RING, 1), i, :].rearrange("p r d -> p (r d)"),
                                            in0=x_in[:, i, :], in1=bo_row[:, :], op=ALU.add) \
                        .then_inc(x_bo_ready, 1)

                def weigh(t):
                    tile = 4 * bs + t - 1
                    if not valid(tile):
                        return
                    pool.wait_ge(exp_ready, tile + 1)
                    e = E[:, (t + 3) % 4, :, :]
                    b_tile = (bs * T + t - 1) % MT
                    nc.gpsimd.tensor_tensor(out=e, in0=e, in1=mask_f[:, bass.ds(b_tile, 1), :]
                                            .broadcast_to((P, H, SK)), op=ALU.mult).then_inc(weighted, 1)

                def normalise(t):
                    tile = 4 * bs + t - 2
                    if not valid(tile):
                        return
                    i = (t + 2) % 4
                    pool.wait_ge(inv_ready, tile + 1)
                    e = E[:, i, :, :]
                    nc.gpsimd.tensor_tensor(out=e, in0=e, in1=inv_sum[:, i, :].unsqueeze(2)
                                            .broadcast_to((P, H, SK)), op=ALU.mult).then_inc(probs_ready, 1)

                def inv_std(i):
                    if not has(bo_):
                        return
                    tile = 4 * bo_ + i
                    pool.wait_ge(stats_ready, tile + 1)
                    nc.gpsimd.tensor_tensor(out=var_eps[:, i:i + 1], in0=mean_var[:, i, 1:2], in1=ln_eps[:, :],
                                            op=ALU.add).then_inc(var_eps_ready, 1)
                    pool.wait_ge(var_eps_ready, tile + 1)
                    nc.gpsimd.tensor_tensor(out=rstd[:, i:i + 1], in0=var_eps[:, i:i + 1],
                                            in1=minus_half[:, :], op=ALU.pow).then_inc(rstd_ready, 1)

                def add_beta(i):
                    if not has(bo_):
                        return
                    pool.wait_ge(scaled, 4 * bo_ + i + 1)
                    nc.gpsimd.tensor_tensor(out=Y[:, i, :], in0=Y[:, i, :], in1=b_row[:, :], op=ALU.add) \
                        .then_inc(normed, 1)

                if isinstance(s, int) and s == 1:
                    pool.wait_ge(mask_ready, 2)
                normalise(0), inv_std(0), weigh(0)
                add_bo(0), inv_std(1), normalise(1), add_bo(1), weigh(1)
                inv_std(2), add_beta(0), normalise(2), add_bo(2), weigh(2), add_beta(1)
                add_bo(3), inv_std(3), normalise(3), add_beta(2), weigh(3), add_beta(3)

            step(0, 0)
            steps(pool, step)


_INPUTS = ["x", "ctx_1024", "mask_1x1xSxS2_if1", "L0_xattn_Wq", "L0_xattn_bq", "L0_xattn_Wk", "L0_xattn_bk",
           "L0_xattn_Wv", "L0_xattn_bv", "L0_xattn_Wo", "L0_xattn_bo", "L0_xattn_ln_g", "L0_xattn_ln_b"]


def kernel(**inputs):
    import concourse.bacc as bacc
    from concourse.bass_utils import run_bass_kernel_spmd

    nc = bacc.Bacc("TRN2", target_bir_lowering=False, num_devices=1, dynamic_dma_scratch_size=1024)
    arrays, args = {}, []
    for name in _INPUTS:
        a = np.ascontiguousarray(inputs[name])
        arrays[f"in_{name}"] = a
        args.append(nc.dram_tensor(f"in_{name}", a.shape, mybir.dt.from_np(a.dtype), kind="ExternalInput").ap())
    out = nc.dram_tensor("out_y", inputs["x"].shape, FP32, kind="ExternalOutput").ap()
    xattn_program(nc, *args, out)
    result = run_bass_kernel_spmd(nc, [arrays], core_ids=[0])
    return result.results[0]["out_y"]
```

```python
from contextlib import ExitStack

import numpy as np

import concourse.bass as bass
from concourse import mybir

FP32 = mybir.dt.float32
FP32R = mybir.dt.float32r
BF16 = mybir.dt.bfloat16
I32 = mybir.dt.int32
ALU = mybir.AluOpType
ACT = mybir.ActivationFunctionType
AX = mybir.AxisListType


def xattn_program(nc, x, ctx, mask, Wq, bq, Wk, bk, Wv, bv, Wo, bo, ln_g, ln_b, out):
    B, S, D = x.shape
    SK = ctx.shape[1]
    H = 16
    DK = D // H
    P = 128
    C = D // P
    HG = H // C
    GK = HG * SK
    T = 4
    ROWS = T * P
    NB = B * S // ROWS
    NT = NB * T
    BB = S // ROWS
    MT = S // P
    HA = 4
    HV = H - HA
    RING = 3
    SCALE = float(np.sqrt(np.float32(DK)))
    NEG = -1e9 * SCALE
    LN_EPS = 1e-5
    SUM_EPS = 1e-9
    STEPS = NB + 3
    LOOP_FROM, LOOP_TO = 3, 3 + (NB - 3) // BB * BB

    x_rows = x.rearrange("b s d -> (b s) d").rearrange("(n p) d -> n p d", p=P)
    out_rows = out.rearrange("b s d -> (b s) d").rearrange("(n p) d -> n p d", p=P)

    es = ExitStack()
    with es:
        def sb(name, shape, dt):
            return es.enter_context(nc.sbuf_tensor(name, shape, dt))

        def sem(name):
            return es.enter_context(nc.semaphore(name))

        ident = sb("ident", [P, P], FP32)
        minus_half = sb("minus_half", [P, 1], FP32)
        ln_eps = sb("ln_eps", [P, 1], FP32)
        WqT_hi = sb("WqT_hi", [P, C, D], FP32R)
        WqT_lo = sb("WqT_lo", [P, C, D], FP32R)
        WoT_hi = sb("WoT_hi", [P, C, D], FP32R)
        WoT_lo = sb("WoT_lo", [P, C, D], FP32R)
        K_hi = sb("K_hi", [P, C, B, SK], FP32R)
        K_lo = sb("K_lo", [P, C, B, SK], FP32R)
        Kd_hi = sb("Kd_hi", [P, C, HG, SK], FP32R)
        Kd_lo = sb("Kd_lo", [P, C, HG, SK], FP32R)
        V_all = sb("V_all", [SK, B, D], FP32)
        V_now = sb("V_now", [SK, D], FP32)
        mask_f = sb("mask_f", [P, MT, SK], FP32)
        mask_bias = sb("mask_bias", [P, MT, SK], BF16)
        qk_bias = sb("qk_bias", [P, 2 * C], FP32)
        bo_row = sb("bo_row", [P, D], FP32)
        g_row = sb("g_row", [P, D], FP32)
        b_row = sb("b_row", [P, D], FP32)

        with nc.sbuf_tensor("WvT_lo", [P, RING, C, D], FP32R) as under_x_bo, \
                nc.sbuf_tensor("WvT_hi", [P, C, D], FP32R) as under_Y:
            WvT_lo, WvT_hi = under_x_bo[:, RING - 1, :, :], under_Y[:, :, :]
        x_bo = sb("x_bo", [P, RING, T, D], FP32)
        Y = sb("Y", [P, T, D], FP32)
        x_in = sb("x_in", [P, T, D], FP32)
        xT_hi = AT_hi = sb("xT_AT_hi", [P, C, ROWS], FP32R)
        xT_lo = AT_lo = sb("xT_AT_lo", [P, C, ROWS], FP32R)
        QT_hi = sb("QT_hi", [P, 2, C, ROWS], FP32R)
        QT_lo = sb("QT_lo", [P, 2, C, ROWS], FP32R)
        E = sb("E", [P, T, H, SK], FP32)
        PT = sb("PT", [P, H, ROWS], FP32)
        rowmax = sb("rowmax", [P, T, H], FP32)
        exp_bias = sb("exp_bias", [P, T, HA], FP32)
        rowsum = sb("rowsum", [P, T, H], FP32)
        rowsum_eps = sb("rowsum_eps", [P, T, H], FP32)
        inv_sum = sb("inv_sum", [P, T, H], FP32)
        bn = sb("bn", [P, T, 6], FP32)
        mean_var = sb("mean_var", [P, T, 2], FP32)
        var_eps = sb("var_eps", [P, T], FP32)
        rstd = sb("rstd", [P, T], FP32)

        W_nat = {n: PT[:, C * i:C * i + C, :] for i, n in enumerate("kvqo")}
        flat = E[:, :, :, :].rearrange("p t h k -> p (t h k)")
        ctx_nat = flat[0:SK, 0:B * D].rearrange("p (b d) -> p b d", b=B)
        qk_nat = flat[0:2 * C, B * D:B * D + P]
        bv_row = V_now[:, :]
        ctxT_hi, ctxT_lo = (w[:, :, :].rearrange("p c d -> p (c d)")[:, 0:C * B * SK]
                            .rearrange("p (c n) -> p c n", c=C) for w in (WoT_hi, WoT_lo))
        W_hi = {"q": WqT_hi, "o": WoT_hi, "k": QT_hi[:, 1, :, :],
                "v": WvT_hi}
        W_lo = {"q": WqT_lo, "o": WoT_lo, "k": QT_lo[:, 1, :, :],
                "v": WvT_lo}
        mask_i = Y[:, :, :].rearrange("p t d -> p (t d)")[:, 0:MT * SK].bitcast(I32) \
            .rearrange("p (t k) -> p t k", t=MT)

        banks = [es.enter_context(nc.psum_tensor(f"bank{i}", [P, 4, 512], FP32)) if i == 0 else
                 es.enter_context(nc.psum_tensor(f"bank{i}", [P, 512], FP32)) for i in (0, 4, 5, 6, 7)]
        scores_ps, pt_ps_bank, *turn_banks = banks

        def prep_bank(n):
            if n >= EARLY:
                return pt_ps_bank[:, :]
            return scores_ps[:, n % 5, :] if n % 5 < 4 else pt_ps_bank[:, :]

        def out_bank(i):
            return turn_banks[i % 3][:, :]

        def xt_bank(i):
            return turn_banks[(T + i) % 3][:, :]

        def q_bank(g):
            return turn_banks[(2 * T + g) % 3][:, :]

        def av_bank(g):
            return turn_banks[(3 * T + g) % 3]

        w_loaded = {n: sem(f"w{n}_loaded") for n in "kvqo"}
        ctx_loaded = sem("ctx_loaded")
        qk_loaded = sem("qk_loaded")
        bv_loaded = sem("bv_loaded")
        bo_loaded = sem("bo_loaded")
        rows_loaded = sem("rows_loaded")
        mask_loaded = sem("mask_loaded")
        ident_zeroed = sem("ident_zeroed")
        ident_ready = sem("ident_ready")
        Kd_zeroed = sem("Kd_zeroed")
        prep_ps = sem("prep_ps")
        prep_act = sem("prep_act")
        prep_dve = sem("prep_dve")
        mask_ready = sem("mask_ready")
        x_loaded = [sem(f"x_loaded{i}") for i in range(T)]
        xt_ps = sem("xt_ps")
        xt_hi = sem("xt_hi")
        xt_lo = sem("xt_lo")
        x_bo_ready = sem("x_bo_ready")
        q_ps = sem("q_ps")
        q_hi = sem("q_hi")
        q_ready = sem("q_ready")
        kd_ready = sem("kd_ready")
        s_ps = sem("s_ps")
        biased = sem("biased")
        max_ready = sem("max_ready")
        exp_bias_ready = sem("exp_bias_ready")
        shifted = sem("shifted")
        exp_ready = sem("exp_ready")
        weighted = sem("weighted")
        sum_ready = sem("sum_ready")
        sum_eps_ready = sem("sum_eps_ready")
        inv_ready = sem("inv_ready")
        probs_ready = sem("probs_ready")
        pt_ps = sem("pt_ps")
        pt_ready = sem("pt_ready")
        v_ready = sem("v_ready")
        av_ps = sem("av_ps")
        at_hi = sem("at_hi")
        at_lo = sem("at_lo")
        out_ps = sem("out_ps")
        y_ready = sem("y_ready")
        bn_ready = sem("bn_ready")
        aggr_turn = sem("aggr_turn")
        stats_ready = sem("stats_ready")
        centered = sem("centered")
        var_eps_ready = sem("var_eps_ready")
        rstd_ready = sem("rstd_ready")
        scaled = sem("scaled")
        normed = sem("normed")
        stored = [sem(f"stored{i}") for i in range(T)]

        block = es.enter_context(nc.Block())

        PREP = ([("bias", None, 0)] + [("wT", "q", c) for c in range(C)] + [("wT", "k", c) for c in range(C)] +
                [("ctxT", None, c) for c in range(C)] + [("K", None, g) for g in range(C)])
        EARLY = len(PREP)
        PREP += ([("wT", "v", c) for c in range(C)] + [("V", None, b) for b in range(B)] +
                 [("wT", "o", c) for c in range(C)])
        FILLS_BEFORE = 1 + C
        FILLS_BEHIND = (0, 0, 0, 2, 6, 2, 2, 0)
        assert FILLS_BEFORE + sum(FILLS_BEHIND) == EARLY and BB == 4

        def fills_behind(unit):
            at = FILLS_BEFORE + sum(FILLS_BEHIND[:unit])
            return range(at, at + FILLS_BEHIND[unit])

        def readers(use):
            return ("act", "dve") if use[0] in ("wT", "ctxT", "K") else ("dve",)

        def prep_count(engine, n):
            return sum(engine in readers(u) for u in PREP[:n])

        def position(kind, w=None):
            return max(n for n, u in enumerate(PREP) if u[:2] == (kind, w)) + 1

        def valid(tile):
            return not isinstance(tile, int) or 0 <= tile < NT

        def has(b):
            return not isinstance(b, int) or 0 <= b < NB

        def steps(engine, step):
            for s in range(1, LOOP_FROM):
                step(s, s % BB)
            with engine.Fori(0, (LOOP_TO - LOOP_FROM) // BB) as i:
                for k in range(LOOP_FROM, LOOP_FROM + BB):
                    step(BB * i + k, k % BB)
            for s in range(LOOP_TO, STEPS):
                step(s, s % BB)

        @block.sync
        def _(sp):
            def load_w(n, w):
                sp.dma_start(W_nat[n], w.rearrange("(i p) d -> p i d", p=P)).then_inc(w_loaded[n], 16)

            def load_row(n, row, vector):
                sp.dma_start(row, vector.rearrange("(a n) -> a n", a=1).broadcast_to((row.shape[0], D))) \
                    .then_inc(n, 16)

            load_w("q", Wq)
            for i in range(T):
                sp.dma_start(x_in[:, i, :], x_rows[i]).then_inc(x_loaded[i], 16)
            load_w("k", Wk)
            sp.dma_start(ctx_nat, ctx.rearrange("b k d -> k b d")).then_inc(ctx_loaded, 16)
            load_row(bo_loaded, bo_row[:, :], bo)
            sp.dma_start(mask_i, mask.rearrange("a b (t p) k -> p (a b t) k", p=P)).then_inc(mask_loaded, 16)
            load_w("v", Wv)
            load_row(bv_loaded, bv_row, bv)
            load_w("o", Wo)
            load_row(rows_loaded, g_row[:, :], ln_g)
            load_row(rows_loaded, b_row[:, :], ln_b)

            def step(s, phase):
                b_out = s - 3
                b_next = s + 1

                def store(i):
                    if has(b_out):
                        sp.wait_ge(normed, 4 * b_out + i + 1)
                        sp.dma_start(out_rows[bass.ds(4 * b_out + i, 1)].rearrange("a p d -> p (a d)"),
                                     Y[:, i, :]).then_inc(stored[i], 16)

                def load(i):
                    if has(s) and has(b_next):
                        sp.wait_ge(xt_ps, 4 * s + i + 1)
                        sp.wait_ge(x_bo_ready, 4 * s + i + 1)
                        sp.dma_start(x_in[:, i, :],
                                     x_rows[bass.ds(4 * b_next + i, 1)].rearrange("a p d -> p (a d)")) \
                            .then_inc(x_loaded[i], 16)

                load(0), load(1), load(2), store(0), store(1), load(3), store(2), store(3)

            step(0, 0)
            steps(sp, step)
            for i in range(T):
                sp.wait_ge(stored[i], 16 * NB)

        @block.tensor
        def _(pe):
            mm = nc.tensor.matmul

            def accumulate(bank, products):
                for n, (a, b) in enumerate(products):
                    last = mm(bank, a, b, start=(n == 0), stop=(n == len(products) - 1))
                return last

            def fill(n):
                kind, w, c = PREP[n]
                bank = prep_bank(n)
                if n >= EARLY:
                    pe.wait_ge(prep_dve, prep_count("dve", n))
                elif n >= 5:
                    pe.wait_ge(prep_dve, prep_count("dve", n - 4))
                if kind == "bias":
                    pe.wait_ge(qk_loaded, 32)
                    last = nc.tensor.transpose(bank[:, 0:2 * C], qk_nat, ident[0:2 * C, 0:2 * C])
                elif kind == "wT":
                    if c == 0:
                        pe.wait_ge(w_loaded[w], 16)
                    for i in range(C):
                        last = nc.tensor.transpose(bank[:, i * P:i * P + P], W_nat[w][:, i, c * P:c * P + P],
                                                   ident[:, :])
                elif kind == "ctxT":
                    if c == 0:
                        pe.wait_ge(ctx_loaded, 16)
                    for b in range(B):
                        last = nc.tensor.transpose(bank[:, b * SK:b * SK + SK],
                                                   ctx_nat[:, b, c * P:c * P + P], ident[0:SK, 0:SK])
                elif kind == "K":
                    pe.wait_ge(prep_dve, prep_count("dve", position("ctxT")))
                    products = [(W_hi["k"][:, k, c * P:c * P + P], ctxT_lo[:, k, :]) for k in range(C)]
                    products += [(W_lo["k"][:, k, c * P:c * P + P], ctxT_hi[:, k, :]) for k in range(C)]
                    products += [(W_hi["k"][:, k, c * P:c * P + P], ctxT_hi[:, k, :]) for k in range(C)]
                    last = accumulate(bank[:, 0:B * SK], products)
                else:
                    pe.wait_ge(prep_dve, prep_count("dve", position("wT", "v")))
                    keys = slice(c * SK, c * SK + SK)
                    products = [(ctxT_hi[:, k, keys], W_lo["v"][:, k, :]) for k in range(C)]
                    products += [(ctxT_lo[:, k, keys], W_hi["v"][:, k, :]) for k in range(C)]
                    products += [(ctxT_hi[:, k, keys], W_hi["v"][:, k, :]) for k in range(C)]
                    last = accumulate(bank[0:SK, :], products)
                last.then_inc(prep_ps, 1)

            def step(s, phase):
                bx, bs, ba, bo_ = s, s - 1, s - 2, s - 3

                def XT(i):
                    if not has(bx):
                        return
                    pe.wait_ge(x_loaded[i], 16 * bx + 16)
                    if i < 3 and has(bo_):
                        pe.wait_ge(y_ready, 4 * bo_ + i + 2)
                    if i == 3:
                        pe.wait_ge(xt_lo, 4 * bx + 1)
                    for k in range(C):
                        last = nc.tensor.transpose(xt_bank(i)[:, k * P:k * P + P], x_in[:, i, k * P:k * P + P],
                                                   ident[:, :])
                    last.then_inc(xt_ps, 1)

                def Q(g):
                    if not has(bx):
                        return
                    if g == 0:
                        pe.wait_ge(xt_lo, 4 * bx + 4)
                    if g == 3:
                        pe.wait_ge(q_ready, 4 * bx + 1)
                    if isinstance(bx, int) and bx == 0:
                        pe.wait_ge(prep_dve, prep_count("dve", position("wT", "q")))
                    last = accumulate(q_bank(g), [(w[:, k, g * P:g * P + P], r[:, k, :])
                                                  for w, r in ((WqT_lo, xT_hi), (WqT_hi, xT_lo), (WqT_hi, xT_hi))
                                                  for k in range(C)])
                    last.then_inc(q_ps, 1)

                def S(t, half):
                    if not has(bs):
                        return
                    tile = 4 * bs + t
                    if t == 0 and half == 0:
                        pe.wait_ge(q_ready, 4 * bs + 4)
                    if not isinstance(tile, int) or tile:
                        pe.wait_ge(biased, 2 * tile - 1 + half)
                    if t == 0 and phase == 1:
                        pe.wait_ge(kd_ready, 2 * (bs // BB) + half + 1)
                    for g in (2 * half, 2 * half + 1):
                        last = accumulate(scores_ps[:, g, 0:GK],
                                          [(q[:, (phase - 1) % 2, g, t * P:t * P + P],
                                            kd[:, g, :, :].rearrange("p j k -> p (j k)"))
                                           for q, kd in ((QT_lo, Kd_hi), (QT_hi, Kd_lo), (QT_hi, Kd_hi))])
                    last.then_inc(s_ps, 1)

                def PTr(t, g):
                    tile = 4 * bs + t - 3
                    if not valid(tile):
                        return
                    if g == 0:
                        pe.wait_ge(probs_ready, tile + 1)
                        if isinstance(tile, int) and tile == 0:
                            pe.wait_ge(prep_dve, prep_count("dve", len(PREP)))
                    if not isinstance(tile, int) or 4 * tile + g:
                        pe.wait_ge(pt_ready, 4 * tile + g)
                    for j in range(HG):
                        last = nc.tensor.transpose(pt_ps_bank[0:SK, j * P:j * P + P],
                                                   E[:, (t + 1) % 4, HG * g + j, :], ident[:, :])
                    last.then_inc(pt_ps, 1)

                def AV(g):
                    if not has(ba):
                        return
                    if g == 0:
                        pe.wait_ge(pt_ready, 16 * ba + 16)
                        if phase == 2:
                            pe.wait_ge(v_ready, ba // BB + 1)
                    if g == 3:
                        pe.wait_ge(at_lo, 4 * ba + 1)
                    elif has(bx):
                        pe.wait_ge(q_ready, 4 * bx + g + 2)
                    elif has(bo_):
                        pe.wait_ge(y_ready, 4 * bo_ + (4, 2, 3)[g])
                    for j in range(HG):
                        h = HG * g + j
                        last = mm(av_bank(g)[DK * j:DK * j + DK, :], V_now[:, DK * h:DK * h + DK],
                                  PT[0:SK, h, :], start=True, stop=True, tile_position=(0, DK * j))
                    last.then_inc(av_ps, 1)

                def OUT(i):
                    if not has(bo_):
                        return
                    if i == 0:
                        pe.wait_ge(at_lo, 4 * bo_ + 4)
                    if i == 3:
                        pe.wait_ge(y_ready, 4 * bo_ + 1)
                    last = accumulate(out_bank(i), [(a[:, k, i * P:i * P + P], w[:, k, :])
                                                    for a, w in ((AT_hi, WoT_lo), (AT_lo, WoT_hi), (AT_hi, WoT_hi))
                                                    for k in range(C)])
                    last.then_inc(out_ps, 1)

                def late(n):
                    if isinstance(s, int) and s == 1:
                        fill(EARLY + n)

                if isinstance(s, int) and s == 0:
                    for unit in range(2 * T):
                        XT(unit) if unit < T else Q(unit - T)
                        for n in fills_behind(unit):
                            fill(n)
                    pe.wait_ge(prep_dve, prep_count("dve", EARLY))
                    return
                late(0), late(1), S(0, 0), S(0, 1), PTr(0, 0), late(2), OUT(0), PTr(0, 1), OUT(1), late(3)
                PTr(0, 2), OUT(2), PTr(0, 3), S(1, 0), S(1, 1), PTr(1, 0), OUT(3), PTr(1, 1), late(4), XT(0)
                XT(1), PTr(1, 2), late(5), S(2, 0), XT(2), late(6), PTr(1, 3), S(2, 1), XT(3), PTr(2, 0)
                late(7), S(3, 0), S(3, 1), late(8), PTr(2, 1), Q(0), late(9), PTr(2, 2), Q(1), late(10)
                PTr(2, 3), Q(2), Q(3), late(11), AV(0), PTr(3, 0), AV(1), PTr(3, 1), AV(2), PTr(3, 2), AV(3)
                PTr(3, 3)

            pe.wait_ge(ident_ready, 1)
            for n in range(FILLS_BEFORE):
                fill(n)
            step(0, 0)
            steps(pe, step)

        @block.scalar
        def _(act):
            cp = nc.scalar.activation
            act.dma_start(qk_nat[0:C, :], bq.rearrange("(g p) -> g p", p=P)).then_inc(qk_loaded, 16)
            act.dma_start(qk_nat[C:2 * C, :], bk.rearrange("(g p) -> g p", p=P)).then_inc(qk_loaded, 16)

            def fill_out(n):
                kind, w, c = PREP[n]
                if "act" not in readers(PREP[n]):
                    return
                bank = prep_bank(n)
                act.wait_ge(prep_ps, n + 1)
                if (kind, w, c) == ("wT", "v", 0):
                    act.wait_ge(mask_ready, 2)
                if kind == "K":
                    last = cp(K_hi[:, c, :, :].rearrange("p b k -> p (b k)"), bank[:, 0:B * SK],
                              ACT.Identity, bias=qk_bias[:, C + c:C + c + 1])
                elif kind == "ctxT":
                    last = cp(ctxT_hi[:, c, :], bank[:, 0:B * SK], ACT.Copy)
                else:
                    last = cp(W_hi[w][:, c, :], bank, ACT.Copy)
                last.then_inc(prep_act, 1)

            def step(s, phase):
                bx, bs, ba, bo_ = s, s - 1, s - 2, s - 3

                def XT_hi(i):
                    if not has(bx):
                        return
                    act.wait_ge(xt_ps, 4 * bx + i + 1)
                    cp(xT_hi[:, :, i * P:i * P + P], xt_bank(i).rearrange("p (k r) -> p k r", k=C),
                       ACT.Copy).then_inc(xt_hi, 1)

                def Q_hi(g):
                    if not has(bx):
                        return
                    act.wait_ge(q_ps, 4 * bx + g + 1)
                    cp(QT_hi[:, phase % 2, g, :], q_bank(g), ACT.Identity, bias=qk_bias[:, g:g + 1]).then_inc(q_hi, 1)

                def K_copy(half):
                    if phase != 0 or not has(s):
                        return
                    if isinstance(s, int) and s == 0:
                        act.wait_ge(prep_dve, prep_count("dve", position("K") - 2 + 2 * half))
                    else:
                        act.wait_ge(s_ps, 8 * s - 1 + half)
                    groups = slice(2 * half, 2 * half + 2)
                    for src, dst in ((K_hi, Kd_hi), (K_lo, Kd_lo)):
                        for j in range(HG):
                            rows = slice(DK * j, DK * j + DK)
                            last = cp(dst[rows, groups, j, :],
                                      src[rows, groups, bass.ds(s // BB, 1), :]
                                      .rearrange("p g b k -> p g (b k)").bitcast(FP32), ACT.Copy)
                    last.then_inc(kd_ready, 1)

                def exponent(t):
                    tile = 4 * bs + t - 1
                    if not valid(tile):
                        return
                    act.wait_ge(shifted, tile + 1)
                    act.wait_ge(exp_bias_ready, tile + 1)
                    i = (t + 3) % 4
                    for h in range(HV, H):
                        cp(E[:, i, h, :], E[:, i, h, :], ACT.Exp, scale=1.0 / SCALE,
                           bias=exp_bias[:, i, h - HV:h - HV + 1])
                    e = E[:, i, 0:HV, :]
                    cp(e, e, ACT.Exp, scale=1.0 / SCALE).then_inc(exp_ready, 1)

                def PT_out(t, g):
                    tile = 4 * bs + t - 3
                    if not valid(tile):
                        return
                    act.wait_ge(pt_ps, 4 * tile + g + 1)
                    i = (t + 1) % 4
                    cp(PT[0:SK, HG * g:HG * g + HG, i * P:i * P + P],
                       pt_ps_bank[0:SK, :].rearrange("p (j r) -> p j r", j=HG), ACT.Copy).then_inc(pt_ready, 1)

                def V_copy():
                    if phase != 2 or not has(ba):
                        return
                    if isinstance(ba, int) and ba == 0:
                        act.wait_ge(prep_dve, prep_count("dve", position("V")))
                    else:
                        act.wait_ge(av_ps, 4 * ba)
                    cp(V_now[:, :], V_all[:, bass.ds(ba // BB, 1), :].rearrange("p b d -> p (b d)"),
                       ACT.Copy).then_inc(v_ready, 1)

                def AV_hi(g):
                    if not has(ba):
                        return
                    act.wait_ge(av_ps, 4 * ba + g + 1)
                    cp(AT_hi[:, g, :], av_bank(g)[:, :], ACT.Copy).then_inc(at_hi, 1)

                def LN_scale(i):
                    if not has(bo_):
                        return
                    act.wait_ge(centered, 4 * bo_ + i + 1)
                    act.wait_ge(rstd_ready, 4 * bo_ + i + 1)
                    cp(Y[:, i, :], Y[:, i, :], ACT.Copy, scale=rstd[:, i:i + 1]).then_inc(scaled, 1)

                def late_hi(n):
                    if isinstance(s, int) and s == 1:
                        fill_out(EARLY + n)

                if isinstance(s, int) and s == 0:
                    act.wait_ge(prep_dve, 1)
                    act.wait_ge(Kd_zeroed, 2)
                    for unit in range(2 * T):
                        XT_hi(unit) if unit < T else Q_hi(unit - T)
                        for n in fills_behind(unit):
                            fill_out(n)
                        if unit in (T + 1, T + 2):
                            K_copy(unit - T - 1)
                    return
                exponent(0), late_hi(0), PT_out(0, 0), PT_out(0, 1), late_hi(1), late_hi(2), PT_out(0, 2)
                late_hi(3), exponent(1), PT_out(0, 3), LN_scale(0), PT_out(1, 0), PT_out(1, 1), XT_hi(0)
                XT_hi(1), PT_out(1, 2), XT_hi(2), PT_out(1, 3), LN_scale(1), XT_hi(3), PT_out(2, 0)
                exponent(2), PT_out(2, 1), late_hi(8), Q_hi(0), PT_out(2, 2), late_hi(9), late_hi(10)
                K_copy(0), Q_hi(1), V_copy(), PT_out(2, 3), LN_scale(2), K_copy(1), Q_hi(2), exponent(3)
                Q_hi(3), late_hi(11), PT_out(3, 0), AV_hi(0), PT_out(3, 1), AV_hi(1), PT_out(3, 2), AV_hi(2)
                AV_hi(3), PT_out(3, 3), LN_scale(3)

            for n in range(FILLS_BEFORE):
                fill_out(n)
            step(0, 0)
            steps(act, step)

        @block.vector
        def _(dve):
            tt = nc.vector.tensor_tensor

            for kd in (Kd_hi, Kd_lo):
                nc.vector.memset(kd[:, :, :, :].bitcast(FP32), 0.0).then_inc(Kd_zeroed, 1)

            def fill_out(n):
                kind, w, c = PREP[n]
                if "dve" not in readers(PREP[n]):
                    return
                bank = prep_bank(n)
                dve.wait_ge(prep_ps, n + 1)
                if kind == "bias":
                    last = nc.vector.tensor_copy(qk_bias[:, :], bank[:, 0:2 * C])
                elif kind == "ctxT":
                    dve.wait_ge(prep_act, prep_count("act", n + 1))
                    last = tt(ctxT_lo[:, c, :], bank[:, 0:B * SK], ctxT_hi[:, c, :].bitcast(FP32), ALU.subtract)
                elif kind == "K":
                    dve.wait_ge(prep_act, prep_count("act", n + 1))
                    last = nc.vector.scalar_tensor_tensor(
                        out=K_lo[:, c, :, :].rearrange("p b k -> p (b k)"), in0=bank[:, 0:B * SK],
                        scalar=qk_bias[:, C + c:C + c + 1],
                        in1=K_hi[:, c, :, :].rearrange("p b k -> p (b k)").bitcast(FP32),
                        op0=ALU.add, op1=ALU.subtract)
                elif kind == "V":
                    dve.wait_ge(bv_loaded, 16)
                    last = tt(V_all[:, c, :], bank[0:SK, :], bv_row, ALU.add)
                else:
                    dve.wait_ge(prep_act, prep_count("act", n + 1))
                    last = tt(W_lo[w][:, c, :], bank, W_hi[w][:, c, :].bitcast(FP32), ALU.subtract)
                last.then_inc(prep_dve, 1)

            def masks():
                dve.wait_ge(mask_loaded, 16)
                nc.vector.tensor_copy(mask_f[:, :, :], mask_i).then_inc(mask_ready, 1)
                dve.wait_ge(mask_ready, 1)
                nc.vector.tensor_scalar(mask_bias[:, :, :], mask_f[:, :, :], 0.0, NEG,
                                        ALU.is_equal, ALU.mult).then_inc(mask_ready, 1)

            def step(s, phase):
                bx, bs, ba, bo_ = s, s - 1, s - 2, s - 3

                def XT_lo(i):
                    if not has(bx):
                        return
                    dve.wait_ge(xt_hi, 4 * bx + i + 1)
                    cols = slice(i * P, i * P + P)
                    tt(xT_lo[:, :, cols], xt_bank(i).rearrange("p (k r) -> p k r", k=C),
                       xT_hi[:, :, cols].bitcast(FP32), ALU.subtract).then_inc(xt_lo, 1)

                def Q_lo(g):
                    if not has(bx):
                        return
                    dve.wait_ge(q_hi, 4 * bx + g + 1)
                    nc.vector.scalar_tensor_tensor(out=QT_lo[:, phase % 2, g, :], in0=q_bank(g),
                                                   scalar=qk_bias[:, g:g + 1],
                                                   in1=QT_hi[:, phase % 2, g, :].bitcast(FP32),
                                                   op0=ALU.add, op1=ALU.subtract).then_inc(q_ready, 1)

                def bias(t, half):
                    tile = 4 * bs + t
                    if not valid(tile):
                        return
                    dve.wait_ge(s_ps, 2 * tile + half + 1)
                    if half == 0 and (not isinstance(tile, int) or tile >= 4):
                        dve.wait_ge(pt_ps, 4 * tile - 12)
                    tt(E[:, t, 2 * HG * half:2 * HG * half + 2 * HG, :].rearrange("p (g j) k -> p g j k", g=2),
                       scores_ps[:, 2 * half:2 * half + 2, 0:GK].rearrange("p g (j k) -> p g j k", j=HG),
                       mask_bias[:, bass.ds(bs % BB * T + t, 1), :].unsqueeze(2).broadcast_to((P, 2, HG, SK)),
                       ALU.add).then_inc(biased, 1)

                def row_max(t):
                    tile = 4 * bs + t
                    if not valid(tile):
                        return
                    dve.wait_ge(biased, 2 * tile + 2)
                    nc.vector.tensor_reduce(out=rowmax[:, t, :], in_=E[:, t, :, :], op=ALU.max, axis=AX.X) \
                        .then_inc(max_ready, 1)

                def shift(t):
                    tile = 4 * bs + t
                    if not valid(tile):
                        return
                    dve.wait_ge(max_ready, tile + 1)
                    nc.vector.tensor_scalar(exp_bias[:, t, :], rowmax[:, t, HV:H], -1.0 / SCALE, None, ALU.mult) \
                        .then_inc(exp_bias_ready, 1)
                    e = E[:, t, 0:HV, :]
                    tt(e, e, rowmax[:, t, 0:HV].unsqueeze(2).broadcast_to((P, HV, SK)), ALU.subtract) \
                        .then_inc(shifted, 1)

                def row_sum(t):
                    tile = 4 * bs + t - 2
                    if not valid(tile):
                        return
                    i = (t + 2) % 4
                    dve.wait_ge(weighted, tile + 1)
                    nc.vector.tensor_reduce(out=rowsum[:, i, :], in_=E[:, i, :, :], op=ALU.add, axis=AX.X) \
                        .then_inc(sum_ready, 1)

                def sum_eps(t):
                    tile = 4 * bs + t - 2
                    if not valid(tile):
                        return
                    i = (t + 2) % 4
                    dve.wait_ge(sum_ready, tile + 1)
                    nc.vector.tensor_scalar(rowsum_eps[:, i, :], rowsum[:, i, :], SUM_EPS, None, ALU.add) \
                        .then_inc(sum_eps_ready, 1)

                def inverse(t):
                    tile = 4 * bs + t - 2
                    if not valid(tile):
                        return
                    i = (t + 2) % 4
                    dve.wait_ge(sum_eps_ready, tile + 1)
                    nc.vector.reciprocal(inv_sum[:, i, :], rowsum_eps[:, i, :]).then_inc(inv_ready, 1)

                def AV_lo(g):
                    if not has(ba):
                        return
                    dve.wait_ge(at_hi, 4 * ba + g + 1)
                    tt(AT_lo[:, g, :], av_bank(g)[:, :], AT_hi[:, g, :].bitcast(FP32), ALU.subtract) \
                        .then_inc(at_lo, 1)

                def residual(i):
                    if not has(bo_):
                        return
                    tile = 4 * bo_ + i
                    dve.wait_ge(out_ps, tile + 1)
                    dve.wait_ge(x_bo_ready, tile + 1)
                    if not isinstance(bo_, int) or bo_:
                        dve.wait_ge(stored[i], 16 * bo_)
                    tt(Y[:, i, :], out_bank(i),
                       x_bo[:, bass.ds(bo_ % RING, 1), i, :].rearrange("p r d -> p (r d)"), ALU.add) \
                        .then_inc(y_ready, 1)

                def stats(i):
                    if not has(bo_):
                        return
                    dve.wait_ge(y_ready, 4 * bo_ + i + 1)
                    nc.vector.bn_stats(bn[:, i, :], Y[:, i, :]).then_inc(bn_ready, 1)

                def aggregate(i):
                    if not has(bo_):
                        return
                    dve.wait_ge(bn_ready, 4 * bo_ + i + 1)
                    dve.sem_inc(aggr_turn, 1)
                    nc.vector.bn_aggr(mean_var[:, i, :], bn[:, i, :]).then_inc(stats_ready, 1)

                def center(i):
                    if not has(bo_):
                        return
                    dve.wait_ge(stats_ready, 4 * bo_ + i + 1)
                    nc.vector.scalar_tensor_tensor(out=Y[:, i, :], in0=Y[:, i, :], scalar=mean_var[:, i, 0:1],
                                                   in1=g_row[:, :], op0=ALU.subtract, op1=ALU.mult) \
                        .then_inc(centered, 1)

                def late_lo(n):
                    if isinstance(s, int) and s == 1:
                        fill_out(EARLY + n)

                if isinstance(s, int) and s == 0:
                    for unit in range(2 * T):
                        XT_lo(unit) if unit < T else Q_lo(unit - T)
                        if unit == 2 * T - 2:
                            masks()
                        for n in fills_behind(unit):
                            fill_out(n)
                    dve.wait_ge(mask_ready, 2)
                    return
                if isinstance(s, int) and s == 2:
                    dve.wait_ge(rows_loaded, 32)
                late_lo(0), row_sum(0), late_lo(1), bias(0, 0), bias(0, 1), sum_eps(0), late_lo(2), row_max(0)
                residual(0), stats(0), inverse(0), aggregate(0), late_lo(3), shift(0), row_sum(1), late_lo(4)
                residual(1), stats(1), center(0), aggregate(1), residual(2), center(1), bias(1, 0), sum_eps(1)
                bias(1, 1), row_max(1), stats(2), late_lo(5), inverse(1), aggregate(2), residual(3), shift(1)
                XT_lo(0), XT_lo(1), late_lo(6), bias(2, 0), bias(2, 1), XT_lo(2), XT_lo(3), late_lo(7)
                row_sum(2), row_max(2), late_lo(8), stats(3), sum_eps(2), aggregate(3), late_lo(9), inverse(2)
                center(2), shift(2), Q_lo(0), center(3), bias(3, 0), late_lo(10), Q_lo(1), row_sum(3)
                bias(3, 1), sum_eps(3), Q_lo(2), row_max(3), inverse(3), Q_lo(3), late_lo(11), AV_lo(0)
                shift(3), AV_lo(1), AV_lo(2), AV_lo(3)

            for n in range(FILLS_BEFORE):
                fill_out(n)
            step(0, 0)
            steps(dve, step)

        @block.gpsimd
        def _(pool):
            nc.gpsimd.memset(ident[:, :], 0.0).then_inc(ident_zeroed, 1)
            nc.gpsimd.memset(minus_half[:, :], -0.5).then_inc(ident_zeroed, 1)
            nc.gpsimd.memset(ln_eps[:, :], LN_EPS).then_inc(ident_zeroed, 1)
            pool.wait_ge(ident_zeroed, 3)
            nc.gpsimd.affine_select(out=ident[:, :], in_=ident[:, :], compare_op=ALU.not_equal, fill=1.0,
                                    base=0, pattern=[[-1, P]], channel_multiplier=1).then_inc(ident_ready, 1)
            pool.wait_ge(bo_loaded, 16)

            def step(s, phase):
                bx, bs, bo_ = s, s - 1, s - 3

                def add_bo(i):
                    if not has(bx):
                        return
                    pool.wait_ge(x_loaded[i], 16 * bx + 16)
                    if not isinstance(bx, int) or bx >= RING:
                        pool.wait_ge(y_ready, 4 * (bx - RING) + i + 1)
                    nc.gpsimd.tensor_tensor(out=x_bo[:, bass.ds(bx % RING, 1), i, :].rearrange("p r d -> p (r d)"),
                                            in0=x_in[:, i, :], in1=bo_row[:, :], op=ALU.add) \
                        .then_inc(x_bo_ready, 1)

                def weigh(t):
                    tile = 4 * bs + t - 1
                    if not valid(tile):
                        return
                    pool.wait_ge(exp_ready, tile + 1)
                    e = E[:, (t + 3) % 4, :, :]
                    b_tile = (bs * T + t - 1) % MT
                    nc.gpsimd.tensor_tensor(out=e, in0=e, in1=mask_f[:, bass.ds(b_tile, 1), :]
                                            .broadcast_to((P, H, SK)), op=ALU.mult).then_inc(weighted, 1)

                def normalise(t):
                    tile = 4 * bs + t - 2
                    if not valid(tile):
                        return
                    i = (t + 2) % 4
                    pool.wait_ge(inv_ready, tile + 1)
                    e = E[:, i, :, :]
                    nc.gpsimd.tensor_tensor(out=e, in0=e, in1=inv_sum[:, i, :].unsqueeze(2)
                                            .broadcast_to((P, H, SK)), op=ALU.mult).then_inc(probs_ready, 1)

                def inv_std(i):
                    if not has(bo_):
                        return
                    tile = 4 * bo_ + i
                    pool.wait_ge(stats_ready, tile + 1)
                    nc.gpsimd.tensor_tensor(out=var_eps[:, i:i + 1], in0=mean_var[:, i, 1:2], in1=ln_eps[:, :],
                                            op=ALU.add).then_inc(var_eps_ready, 1)
                    pool.wait_ge(var_eps_ready, tile + 1)
                    nc.gpsimd.tensor_tensor(out=rstd[:, i:i + 1], in0=var_eps[:, i:i + 1],
                                            in1=minus_half[:, :], op=ALU.pow).then_inc(rstd_ready, 1)

                def add_beta(i):
                    if not has(bo_):
                        return
                    pool.wait_ge(scaled, 4 * bo_ + i + 1)
                    nc.gpsimd.tensor_tensor(out=Y[:, i, :], in0=Y[:, i, :], in1=b_row[:, :], op=ALU.add) \
                        .then_inc(normed, 1)

                if isinstance(s, int) and s == 1:
                    pool.wait_ge(mask_ready, 2)
                if isinstance(s, int) and s == 2:
                    pool.wait_ge(prep_ps, position("V"))
                    pool.wait_ge(rows_loaded, 32)
                weigh(0), inv_std(0), normalise(0), inv_std(1), weigh(1), normalise(1), add_beta(0)
                inv_std(2), add_beta(1), add_bo(0), add_bo(1), add_bo(2), weigh(2), normalise(2), add_bo(3)
                inv_std(3), weigh(3), normalise(3), add_beta(2), add_beta(3)

            step(0, 0)
            steps(pool, step)


_INPUTS = ["x", "ctx_1024", "mask_1x1xSxS2_if1", "L0_xattn_Wq", "L0_xattn_bq", "L0_xattn_Wk", "L0_xattn_bk",
           "L0_xattn_Wv", "L0_xattn_bv", "L0_xattn_Wo", "L0_xattn_bo", "L0_xattn_ln_g", "L0_xattn_ln_b"]


def kernel(**inputs):
    import concourse.bacc as bacc
    from concourse.bass_utils import run_bass_kernel_spmd

    nc = bacc.Bacc("TRN2", target_bir_lowering=False, num_devices=1, dynamic_dma_scratch_size=1024)
    arrays, args = {}, []
    for name in _INPUTS:
        a = np.ascontiguousarray(inputs[name])
        arrays[f"in_{name}"] = a
        args.append(nc.dram_tensor(f"in_{name}", a.shape, mybir.dt.from_np(a.dtype), kind="ExternalInput").ap())
    out = nc.dram_tensor("out_y", inputs["x"].shape, FP32, kind="ExternalOutput").ap()
    xattn_program(nc, *args, out)
    result = run_bass_kernel_spmd(nc, [arrays], core_ids=[0])
    return result.results[0]["out_y"]
```

```python
from contextlib import ExitStack

import numpy as np

import concourse.bass as bass
from concourse import mybir

FP32 = mybir.dt.float32
FP32R = mybir.dt.float32r
BF16 = mybir.dt.bfloat16
I32 = mybir.dt.int32
ALU = mybir.AluOpType
ACT = mybir.ActivationFunctionType
AX = mybir.AxisListType


def xattn_program(nc, x, ctx, mask, Wq, bq, Wk, bk, Wv, bv, Wo, bo, ln_g, ln_b, out):
    B, S, D = x.shape
    SK = ctx.shape[1]
    H = 16
    DK = D // H
    P = 128
    C = D // P
    HG = H // C
    GK = HG * SK
    T = 4
    ROWS = T * P
    NB = B * S // ROWS
    NT = NB * T
    BB = S // ROWS
    MT = S // P
    HA = 4
    HV = H - HA
    RING = 3
    SCALE = float(np.sqrt(np.float32(DK)))
    NEG = -1e9 * SCALE
    LN_EPS = 1e-5
    SUM_EPS = 1e-9
    STEPS = NB + 3
    LOOP_FROM, LOOP_TO = 3, 3 + (NB - 3) // BB * BB

    x_rows = x.rearrange("b s d -> (b s) d").rearrange("(n p) d -> n p d", p=P)
    out_rows = out.rearrange("b s d -> (b s) d").rearrange("(n p) d -> n p d", p=P)

    es = ExitStack()
    with es:
        def sb(name, shape, dt):
            return es.enter_context(nc.sbuf_tensor(name, shape, dt))

        def sem(name):
            return es.enter_context(nc.semaphore(name))

        ident = sb("ident", [P, P], FP32)
        minus_half = sb("minus_half", [P, 1], FP32)
        ln_eps = sb("ln_eps", [P, 1], FP32)
        WqT_hi = sb("WqT_hi", [P, C, D], FP32R)
        WqT_lo = sb("WqT_lo", [P, C, D], FP32R)
        WoT_hi = sb("WoT_hi", [P, C, D], FP32R)
        WoT_lo = sb("WoT_lo", [P, C, D], FP32R)
        K_hi = sb("K_hi", [P, C, B, SK], FP32R)
        K_lo = sb("K_lo", [P, C, B, SK], FP32R)
        Kd_hi = sb("Kd_hi", [P, C, HG, SK], FP32R)
        Kd_lo = sb("Kd_lo", [P, C, HG, SK], FP32R)
        V_all = sb("V_all", [SK, B, D], FP32)
        V_now = sb("V_now", [SK, D], FP32)
        mask_f = sb("mask_f", [P, MT, SK], FP32)
        mask_bias = sb("mask_bias", [P, MT, SK], BF16)
        qk_bias = sb("qk_bias", [P, 2 * C], FP32)
        bo_row = sb("bo_row", [P, D], FP32)
        g_row = sb("g_row", [P, D], FP32)
        b_row = sb("b_row", [P, D], FP32)

        with nc.sbuf_tensor("WvT_lo", [P, RING, C, D], FP32R) as under_x_bo, \
                nc.sbuf_tensor("WvT_hi", [P, C, D], FP32R) as under_Y:
            WvT_lo, WvT_hi = under_x_bo[:, RING - 1, :, :], under_Y[:, :, :]
        x_bo = sb("x_bo", [P, RING, T, D], FP32)
        Y = sb("Y", [P, T, D], FP32)
        x_in = sb("x_in", [P, T, D], FP32)
        xT_hi = AT_hi = sb("xT_AT_hi", [P, C, ROWS], FP32R)
        xT_lo = AT_lo = sb("xT_AT_lo", [P, C, ROWS], FP32R)
        QT_hi = sb("QT_hi", [P, 2, C, ROWS], FP32R)
        QT_lo = sb("QT_lo", [P, 2, C, ROWS], FP32R)
        E = sb("E", [P, T, H, SK], FP32)
        PT = sb("PT", [P, H, ROWS], FP32)
        rowmax = sb("rowmax", [P, T, H], FP32)
        exp_bias = sb("exp_bias", [P, T, HA], FP32)
        rowsum = sb("rowsum", [P, T, H], FP32)
        rowsum_eps = sb("rowsum_eps", [P, T, H], FP32)
        inv_sum = sb("inv_sum", [P, T, H], FP32)
        bn = sb("bn", [P, T, 6], FP32)
        mean_var = sb("mean_var", [P, T, 2], FP32)
        var_eps = sb("var_eps", [P, T], FP32)
        rstd = sb("rstd", [P, T], FP32)

        W_nat = {n: PT[:, C * i:C * i + C, :] for i, n in enumerate("kvqo")}
        flat = E[:, :, :, :].rearrange("p t h k -> p (t h k)")
        ctx_nat = flat[0:SK, 0:B * D].rearrange("p (b d) -> p b d", b=B)
        qk_nat = flat[0:2 * C, B * D:B * D + P]
        bv_row = V_now[:, :]
        VT = PT[:, 0:C, 0:B * SK]
        ctxT_hi, ctxT_lo = (w[:, :, :].rearrange("p c d -> p (c d)")[:, 0:C * B * SK]
                            .rearrange("p (c n) -> p c n", c=C) for w in (WoT_hi, WoT_lo))
        W_hi = {"q": WqT_hi, "o": WoT_hi, "k": QT_hi[:, 1, :, :],
                "v": WvT_hi}
        W_lo = {"q": WqT_lo, "o": WoT_lo, "k": QT_lo[:, 1, :, :],
                "v": WvT_lo}
        mask_i = Y[:, :, :].rearrange("p t d -> p (t d)")[:, 0:MT * SK].bitcast(I32) \
            .rearrange("p (t k) -> p t k", t=MT)

        banks = [es.enter_context(nc.psum_tensor(f"bank{i}", [P, 4, 512], FP32)) if i == 0 else
                 es.enter_context(nc.psum_tensor(f"bank{i}", [P, 512], FP32)) for i in (0, 4, 5, 6, 7)]
        scores_ps, pt_ps_bank, *turn_banks = banks

        def prep_bank(n):
            if n >= EARLY:
                k = n - EARLY
                return turn_banks[0][:, :] if k < LATE_IN_TURN and k % 2 else pt_ps_bank[:, :]
            return scores_ps[:, n % 5, :] if n % 5 < 4 else pt_ps_bank[:, :]

        def pt_depth(s):
            return 4 if isinstance(s, int) and s == NB + 1 else 1

        def pt_bank(s, g):
            return scores_ps[:, g, :] if pt_depth(s) == 4 else pt_ps_bank[:, :]

        def out_bank(i):
            return turn_banks[i % 3][:, :]

        def xt_bank(i):
            return turn_banks[(T + i) % 3][:, :]

        def q_bank(g):
            return turn_banks[(2 * T + g) % 3][:, :]

        def av_bank(g):
            return turn_banks[(3 * T + g) % 3]

        w_loaded = {n: [sem(f"w{n}_loaded{i}") for i in range(C)] for n in "kvqo"}
        ctx_loaded = sem("ctx_loaded")
        qk_loaded = sem("qk_loaded")
        bv_loaded = sem("bv_loaded")
        bo_loaded = sem("bo_loaded")
        rows_loaded = sem("rows_loaded")
        mask_loaded = sem("mask_loaded")
        ident_zeroed = sem("ident_zeroed")
        ident_ready = sem("ident_ready")
        Kd_zeroed = sem("Kd_zeroed")
        prep_ps = sem("prep_ps")
        prep_act = sem("prep_act")
        prep_dve = sem("prep_dve")
        mask_ready = sem("mask_ready")
        x_loaded = [sem(f"x_loaded{i}") for i in range(T)]
        xt_ps = sem("xt_ps")
        xt_hi = sem("xt_hi")
        xt_lo = sem("xt_lo")
        x_bo_ready = sem("x_bo_ready")
        q_ps = sem("q_ps")
        q_hi = sem("q_hi")
        q_ready = sem("q_ready")
        kd_ready = sem("kd_ready")
        s_ps = sem("s_ps")
        biased = sem("biased")
        max_ready = sem("max_ready")
        exp_bias_ready = sem("exp_bias_ready")
        shifted = sem("shifted")
        exp_ready = sem("exp_ready")
        weighted = sem("weighted")
        sum_ready = sem("sum_ready")
        sum_eps_ready = sem("sum_eps_ready")
        inv_ready = sem("inv_ready")
        probs_ready = sem("probs_ready")
        pt_ps = sem("pt_ps")
        pt_ready = sem("pt_ready")
        v_ready = sem("v_ready")
        av_ps = sem("av_ps")
        at_hi = sem("at_hi")
        at_lo = sem("at_lo")
        out_ps = sem("out_ps")
        y_ready = sem("y_ready")
        bn_ready = sem("bn_ready")
        aggr_turn = sem("aggr_turn")
        stats_ready = sem("stats_ready")
        centered = sem("centered")
        var_eps_ready = sem("var_eps_ready")
        rstd_ready = sem("rstd_ready")
        scaled = sem("scaled")
        normed = sem("normed")
        finished = sem("finished")
        stored = [sem(f"stored{i}") for i in range(T)]

        block = es.enter_context(nc.Block())

        PREP = ([("bias", None, 0)] + [("wT", "q", i) for i in range(C)] + [("ctxT", None, c) for c in range(C)] +
                [("wT", "k", i) for i in range(C)] + [("K", None, g) for g in range(C)])
        EARLY = len(PREP)
        PREP += ([("wT", "v", i) for i in range(C)] + [("VT", None, g) for g in range(C)] +
                 [("V", None, b) for b in range(B)] +
                 [("wT", "o", i) for i in range(C)])
        LATE_IN_TURN = 2 * C
        FILLS_BEHIND = (2, 0, 0, 3, 4, 4, 4, 0)
        assert sum(FILLS_BEHIND) == EARLY and BB == 4

        def fills_behind(unit):
            at = sum(FILLS_BEHIND[:unit])
            return range(at, at + FILLS_BEHIND[unit])

        def readers(use):
            return {"bias": ("dve",), "V": ("dve",), "VT": ("act",)}.get(use[0], ("act", "dve"))

        def prep_count(engine, n):
            return sum(engine in readers(u) for u in PREP[:n])

        def dve_count(kind, w, c):
            return prep_count("dve", PREP.index((kind, w, c)) + 1)

        def valid(tile):
            return not isinstance(tile, int) or 0 <= tile < NT

        def has(b):
            return not isinstance(b, int) or 0 <= b < NB

        def is_last(s, i):
            return isinstance(s, int) and s == STEPS - 1 and i == T - 1

        def steps(engine, step):
            for s in range(1, LOOP_FROM):
                step(s, s % BB)
            with engine.Fori(0, (LOOP_TO - LOOP_FROM) // BB) as i:
                for k in range(LOOP_FROM, LOOP_FROM + BB):
                    step(BB * i + k, k % BB)
            for s in range(LOOP_TO, STEPS):
                step(s, s % BB)

        @block.sync
        def _(sp):
            def load_w(n, w, i):
                sp.dma_start(W_nat[n][:, i, :], w[i * P:i * P + P, :]).then_inc(w_loaded[n][i], 16)

            def load_x(i):
                sp.dma_start(x_in[:, i, :], x_rows[i]).then_inc(x_loaded[i], 16)

            def load_row(n, row, vector):
                sp.dma_start(row, vector.rearrange("(a n) -> a n", a=1).broadcast_to((row.shape[0], D))) \
                    .then_inc(n, 16)

            load_x(0), load_w("q", Wq, 0), load_x(1), load_x(2), load_x(3)
            for i in range(1, C):
                load_w("q", Wq, i)
            sp.dma_start(ctx_nat, ctx.rearrange("b k d -> k b d")).then_inc(ctx_loaded, 16)
            for i in range(C):
                load_w("k", Wk, i)
            load_row(bo_loaded, bo_row[:, :], bo)
            sp.dma_start(mask_i, mask.rearrange("a b (t p) k -> p (a b t) k", p=P)).then_inc(mask_loaded, 16)
            for i in range(C):
                load_w("v", Wv, i)
            load_row(bv_loaded, bv_row, bv)
            for i in range(C):
                load_w("o", Wo, i)
            load_row(rows_loaded, g_row[:, :], ln_g)
            load_row(rows_loaded, b_row[:, :], ln_b)

            def step(s, phase):
                b_out = s - 3
                b_next = s + 1

                def store(i):
                    if has(b_out):
                        if is_last(s, i):
                            sp.wait_ge(finished, 1)
                        else:
                            sp.wait_ge(normed, 4 * b_out + i + 1)
                        sp.dma_start(out_rows[bass.ds(4 * b_out + i, 1)].rearrange("a p d -> p (a d)"),
                                     Y[:, i, :]).then_inc(stored[i], 16)

                def load(i):
                    if has(s) and has(b_next):
                        sp.wait_ge(xt_ps, 4 * s + i + 1)
                        sp.wait_ge(x_bo_ready, 4 * s + i + 1)
                        sp.dma_start(x_in[:, i, :],
                                     x_rows[bass.ds(4 * b_next + i, 1)].rearrange("a p d -> p (a d)")) \
                            .then_inc(x_loaded[i], 16)

                load(0), load(1), load(2), store(0), store(1), load(3), store(2), store(3)

            step(0, 0)
            steps(sp, step)
            for i in range(T):
                sp.wait_ge(stored[i], 16 + 16 * NB)

        @block.tensor
        def _(pe):
            mm = nc.tensor.matmul

            def accumulate(bank, products):
                for n, (a, b) in enumerate(products):
                    last = mm(bank, a, b, start=(n == 0), stop=(n == len(products) - 1))
                return last

            def fill(n):
                kind, w, c = PREP[n]
                bank = prep_bank(n)
                k = n - EARLY
                if k < 0:
                    before = n - 5
                elif k < LATE_IN_TURN:
                    before = n - 2 if k >= 2 else EARLY - 1
                else:
                    before = n - 2 if k == LATE_IN_TURN else n - 1
                if k == 1:
                    pe.wait_ge(q_ready, 2)
                if before >= 0 and PREP[before][0] == "VT":
                    pe.wait_ge(prep_act, prep_count("act", before + 1))
                elif before >= 0:
                    pe.wait_ge(prep_dve, prep_count("dve", before + 1))
                if kind == "bias":
                    pe.wait_ge(qk_loaded, 32)
                    last = nc.tensor.transpose(bank[:, 0:2 * C], qk_nat, ident[0:2 * C, 0:2 * C])
                elif kind == "wT":
                    pe.wait_ge(w_loaded[w][c], 16)
                    for k in range(C):
                        last = nc.tensor.transpose(bank[:, k * P:k * P + P], W_nat[w][:, c, k * P:k * P + P],
                                                   ident[:, :])
                elif kind == "ctxT":
                    if c == 0:
                        pe.wait_ge(ctx_loaded, 16)
                    for b in range(B):
                        last = nc.tensor.transpose(bank[:, b * SK:b * SK + SK],
                                                   ctx_nat[:, b, c * P:c * P + P], ident[0:SK, 0:SK])
                elif kind == "K":
                    pe.wait_ge(prep_dve, max(dve_count("ctxT", None, C - 1), dve_count("wT", "k", c)))
                    products = [(W_hi["k"][:, k, c * P:c * P + P], ctxT_lo[:, k, :]) for k in range(C)]
                    products += [(W_lo["k"][:, k, c * P:c * P + P], ctxT_hi[:, k, :]) for k in range(C)]
                    products += [(W_hi["k"][:, k, c * P:c * P + P], ctxT_hi[:, k, :]) for k in range(C)]
                    last = accumulate(bank[:, 0:B * SK], products)
                elif kind == "VT":
                    pe.wait_ge(prep_dve, dve_count("wT", "v", c))
                    products = [(W_hi["v"][:, k, c * P:c * P + P], ctxT_lo[:, k, :]) for k in range(C)]
                    products += [(W_lo["v"][:, k, c * P:c * P + P], ctxT_hi[:, k, :]) for k in range(C)]
                    products += [(W_hi["v"][:, k, c * P:c * P + P], ctxT_hi[:, k, :]) for k in range(C)]
                    last = accumulate(bank[:, 0:B * SK], products)
                else:
                    pe.wait_ge(prep_act, prep_count("act", PREP.index(("VT", None, C - 1)) + 1))
                    for g in range(C):
                        last = nc.tensor.transpose(bank[0:SK, g * P:g * P + P], VT[:, g, c * SK:c * SK + SK],
                                                   ident[:, :])
                last.then_inc(prep_ps, 1)

            def step(s, phase):
                bx, bs, ba, bo_ = s, s - 1, s - 2, s - 3

                def XT(i):
                    if not has(bx):
                        return
                    pe.wait_ge(x_loaded[i], 16 * bx + 16)
                    if i < 3 and has(bo_):
                        pe.wait_ge(y_ready, 4 * bo_ + i + 2)
                    elif i < 3 and bx:
                        pe.wait_ge(q_ready, 4 * bx)
                    if isinstance(bx, int) and bx == 1 and i == 2:
                        pe.wait_ge(prep_act, prep_count("act", EARLY + LATE_IN_TURN))
                    if i == 3:
                        pe.wait_ge(xt_lo, 4 * bx + 1)
                    for k in range(C):
                        last = nc.tensor.transpose(xt_bank(i)[:, k * P:k * P + P], x_in[:, i, k * P:k * P + P],
                                                   ident[:, :])
                    last.then_inc(xt_ps, 1)

                def Q(g):
                    if not has(bx):
                        return
                    if g == 0:
                        pe.wait_ge(xt_lo, 4 * bx + 4)
                    if g == 3:
                        pe.wait_ge(q_ready, 4 * bx + 1)
                    if isinstance(bx, int) and bx == 0:
                        pe.wait_ge(prep_dve, dve_count("wT", "q", g))
                    last = accumulate(q_bank(g), [(w[:, k, g * P:g * P + P], r[:, k, :])
                                                  for w, r in ((WqT_lo, xT_hi), (WqT_hi, xT_lo), (WqT_hi, xT_hi))
                                                  for k in range(C)])
                    last.then_inc(q_ps, 1)

                def S(t, half):
                    if not has(bs):
                        return
                    tile = 4 * bs + t
                    if t == 0 and half == 0:
                        pe.wait_ge(q_ready, 4 * bs + 4)
                    if not isinstance(tile, int) or tile:
                        pe.wait_ge(biased, 2 * tile - 1 + half)
                    if t == 0 and phase == 1:
                        pe.wait_ge(kd_ready, 2 * (bs // BB) + half + 1)
                    for g in (2 * half, 2 * half + 1):
                        last = accumulate(scores_ps[:, g, 0:GK],
                                          [(q[:, (phase - 1) % 2, g, t * P:t * P + P],
                                            kd[:, g, :, :].rearrange("p j k -> p (j k)"))
                                           for q, kd in ((QT_lo, Kd_hi), (QT_hi, Kd_lo), (QT_hi, Kd_hi))])
                    last.then_inc(s_ps, 1)

                def PTr(t, g):
                    tile = 4 * bs + t - 3
                    if not valid(tile):
                        return
                    if g == 0:
                        pe.wait_ge(probs_ready, tile + 1)
                        if isinstance(tile, int) and tile == 0:
                            pe.wait_ge(prep_dve, prep_count("dve", len(PREP)))
                    if pt_depth(s) == 1 and (not isinstance(tile, int) or tile or g):
                        pe.wait_ge(pt_ready, 4 * tile + g)
                    elif pt_depth(s) == 4:
                        if t == 0:
                            pe.wait_ge(biased, 2 * NT)
                        else:
                            pe.wait_ge(pt_ready, 4 * tile + g - 3)
                    for j in range(HG):
                        last = nc.tensor.transpose(pt_bank(s, g)[0:SK, j * P:j * P + P],
                                                   E[:, (t + 1) % 4, HG * g + j, :], ident[:, :])
                    last.then_inc(pt_ps, 1)

                def AV(g):
                    if not has(ba):
                        return
                    if g == 0:
                        pe.wait_ge(pt_ready, 16 * ba + 16)
                        if phase == 2:
                            pe.wait_ge(v_ready, ba // BB + 1)
                    if g == 3:
                        pe.wait_ge(at_lo, 4 * ba + 1)
                    elif has(bx):
                        pe.wait_ge(q_ready, 4 * bx + g + 2)
                    elif has(bo_):
                        pe.wait_ge(y_ready, 4 * bo_ + (4, 2, 3)[g])
                    for j in range(HG):
                        h = HG * g + j
                        last = mm(av_bank(g)[DK * j:DK * j + DK, :], V_now[:, DK * h:DK * h + DK],
                                  PT[0:SK, h, :], start=True, stop=True, tile_position=(0, DK * j))
                    last.then_inc(av_ps, 1)

                def OUT(i):
                    if not has(bo_):
                        return
                    if i == 0:
                        pe.wait_ge(at_lo, 4 * bo_ + 4)
                    if i == 3:
                        pe.wait_ge(y_ready, 4 * bo_ + 1)
                    last = accumulate(out_bank(i), [(a[:, k, i * P:i * P + P], w[:, k, :])
                                                    for a, w in ((AT_hi, WoT_lo), (AT_lo, WoT_hi), (AT_hi, WoT_hi))
                                                    for k in range(C)])
                    last.then_inc(out_ps, 1)

                def late(n):
                    fill(EARLY + n)

                if isinstance(s, int) and s == 0:
                    for unit in range(2 * T):
                        XT(unit) if unit < T else Q(unit - T)
                        for n in fills_behind(unit):
                            fill(n)
                    pe.wait_ge(prep_dve, prep_count("dve", EARLY))
                    return
                if isinstance(s, int) and s == 1:
                    late(0), late(1), S(0, 0), late(2), S(0, 1), late(3), XT(0), S(1, 0), late(4), S(1, 1)
                    late(5), late(6), late(7), S(2, 0), late(8), XT(1), XT(2), late(9), XT(3), late(10)
                    S(2, 1), late(11), S(3, 0), late(12), Q(0), late(13), Q(1), late(14), Q(2), late(15), Q(3)
                    PTr(3, 0), S(3, 1), PTr(3, 1), PTr(3, 2), PTr(3, 3)
                    return
                if isinstance(s, int) and s == 2:
                    XT(0), S(0, 0), PTr(0, 0), XT(1), S(0, 1), PTr(0, 1), XT(2), XT(3), PTr(0, 2), S(1, 0)
                    S(1, 1), PTr(0, 3), Q(0), PTr(1, 0), Q(1), PTr(1, 1), S(2, 0), PTr(1, 2), S(2, 1)
                    PTr(1, 3), Q(2), PTr(2, 0), PTr(2, 1), S(3, 0), PTr(2, 2), S(3, 1), PTr(2, 3), Q(3), AV(0)
                    PTr(3, 0), AV(1), PTr(3, 1), AV(2), PTr(3, 2), AV(3), PTr(3, 3)
                    return
                if isinstance(s, int) and s == NB:
                    S(0, 0), PTr(0, 0), S(0, 1), PTr(0, 1), OUT(0), PTr(0, 2), S(1, 0), PTr(0, 3), OUT(1)
                    PTr(1, 0), S(1, 1), PTr(1, 1), OUT(2), PTr(1, 2), S(2, 0), PTr(1, 3), OUT(3), PTr(2, 0)
                    S(2, 1), PTr(2, 1), S(3, 0), PTr(2, 2), S(3, 1), PTr(2, 3), AV(0), PTr(3, 0), AV(1)
                    PTr(3, 1), AV(2), PTr(3, 2), AV(3), PTr(3, 3)
                    return
                if isinstance(s, int) and s == NB + 1:
                    PTr(0, 0), PTr(0, 1), PTr(0, 2), PTr(0, 3), OUT(0), OUT(1), OUT(2), OUT(3), PTr(1, 0)
                    PTr(1, 1), PTr(1, 2), PTr(1, 3), PTr(2, 0), PTr(2, 1), PTr(2, 2), PTr(2, 3), AV(0), AV(1)
                    AV(2), AV(3)
                    return
                if isinstance(s, int) and s == NB + 2:
                    OUT(0), OUT(1), OUT(2), OUT(3)
                    return
                S(0, 0), S(0, 1), PTr(0, 0), OUT(0), PTr(0, 1), S(1, 0), S(1, 1), PTr(0, 2), OUT(1), PTr(0, 3)
                OUT(2), PTr(1, 0), OUT(3), PTr(1, 1), XT(0), XT(1), PTr(1, 2), XT(2), S(2, 0), PTr(1, 3)
                XT(3), S(2, 1), S(3, 0), PTr(2, 0), Q(0), PTr(2, 1), Q(1), PTr(2, 2), Q(2), S(3, 1), PTr(2, 3)
                Q(3), AV(0), PTr(3, 0), AV(1), PTr(3, 1), AV(2), PTr(3, 2), AV(3), PTr(3, 3)

            pe.wait_ge(ident_ready, 1)
            step(0, 0)
            steps(pe, step)

        @block.scalar
        def _(act):
            cp = nc.scalar.activation
            act.dma_start(qk_nat[0:C, :], bq.rearrange("(g p) -> g p", p=P)).then_inc(qk_loaded, 16)
            act.dma_start(qk_nat[C:2 * C, :], bk.rearrange("(g p) -> g p", p=P)).then_inc(qk_loaded, 16)

            act.wait_ge(ident_zeroed, 3)
            cp(rstd[:, 0:1], minus_half[:, :], ACT.Exp)

            def fill_out(n):
                kind, w, c = PREP[n]
                if "act" not in readers(PREP[n]):
                    return
                bank = prep_bank(n)
                act.wait_ge(prep_ps, n + 1)
                if (kind, w, c) == ("wT", "v", 0):
                    act.wait_ge(mask_ready, 2)
                if kind == "K":
                    last = cp(K_hi[:, c, :, :].rearrange("p b k -> p (b k)"), bank[:, 0:B * SK],
                              ACT.Identity, bias=qk_bias[:, C + c:C + c + 1])
                elif kind == "VT":
                    last = cp(VT[:, c, :], bank[:, 0:B * SK], ACT.Copy)
                elif kind == "ctxT":
                    last = cp(ctxT_hi[:, c, :], bank[:, 0:B * SK], ACT.Copy)
                else:
                    last = cp(W_hi[w][:, :, c * P:c * P + P], bank.rearrange("p (k r) -> p k r", k=C), ACT.Copy)
                last.then_inc(prep_act, 1)

            def step(s, phase):
                bx, bs, ba, bo_ = s, s - 1, s - 2, s - 3

                def XT_hi(i):
                    if not has(bx):
                        return
                    act.wait_ge(xt_ps, 4 * bx + i + 1)
                    cp(xT_hi[:, :, i * P:i * P + P], xt_bank(i).rearrange("p (k r) -> p k r", k=C),
                       ACT.Copy).then_inc(xt_hi, 1)

                def Q_hi(g):
                    if not has(bx):
                        return
                    act.wait_ge(q_ps, 4 * bx + g + 1)
                    cp(QT_hi[:, phase % 2, g, :], q_bank(g), ACT.Identity, bias=qk_bias[:, g:g + 1]).then_inc(q_hi, 1)

                def K_copy(half):
                    if phase != 0 or not has(s):
                        return
                    if isinstance(s, int) and s == 0:
                        act.wait_ge(prep_dve, dve_count("K", None, 2 * half + 1))
                    else:
                        act.wait_ge(s_ps, 8 * s - 1 + half)
                    groups = slice(2 * half, 2 * half + 2)
                    for src, dst in ((K_hi, Kd_hi), (K_lo, Kd_lo)):
                        for j in range(HG):
                            rows = slice(DK * j, DK * j + DK)
                            last = cp(dst[rows, groups, j, :],
                                      src[rows, groups, bass.ds(s // BB, 1), :]
                                      .rearrange("p g b k -> p g (b k)").bitcast(FP32), ACT.Copy)
                    last.then_inc(kd_ready, 1)

                def exponent(t):
                    tile = 4 * bs + t - 1
                    if not valid(tile):
                        return
                    act.wait_ge(shifted, tile + 1)
                    act.wait_ge(exp_bias_ready, tile + 1)
                    i = (t + 3) % 4
                    for h in range(HV, H):
                        cp(E[:, i, h, :], E[:, i, h, :], ACT.Exp, scale=1.0 / SCALE,
                           bias=exp_bias[:, i, h - HV:h - HV + 1])
                    e = E[:, i, 0:HV, :]
                    cp(e, e, ACT.Exp, scale=1.0 / SCALE).then_inc(exp_ready, 1)

                def PT_out(t, g):
                    tile = 4 * bs + t - 3
                    if not valid(tile):
                        return
                    act.wait_ge(pt_ps, 4 * tile + g + 1)
                    i = (t + 1) % 4
                    cp(PT[0:SK, HG * g:HG * g + HG, i * P:i * P + P],
                       pt_bank(s, g)[0:SK, :].rearrange("p (j r) -> p j r", j=HG), ACT.Copy).then_inc(pt_ready, 1)

                def V_copy():
                    if phase != 2 or not has(ba):
                        return
                    if isinstance(ba, int) and ba == 0:
                        act.wait_ge(prep_dve, dve_count("V", None, B - 1))
                    else:
                        act.wait_ge(av_ps, 4 * ba)
                    cp(V_now[:, :], V_all[:, bass.ds(ba // BB, 1), :].rearrange("p b d -> p (b d)"),
                       ACT.Copy).then_inc(v_ready, 1)

                def AV_hi(g):
                    if not has(ba):
                        return
                    act.wait_ge(av_ps, 4 * ba + g + 1)
                    cp(AT_hi[:, g, :], av_bank(g)[:, :], ACT.Copy).then_inc(at_hi, 1)

                def LN_scale(i):
                    if not has(bo_):
                        return
                    act.wait_ge(centered, 4 * bo_ + i + 1)
                    act.wait_ge(rstd_ready, 4 * bo_ + i + 1)
                    cp(Y[:, i, :], Y[:, i, :], ACT.Copy, scale=rstd[:, i:i + 1]).then_inc(scaled, 1)

                def late_hi(n):
                    fill_out(EARLY + n)

                if isinstance(s, int) and s == 0:
                    act.wait_ge(Kd_zeroed, 2)
                    for unit in range(2 * T):
                        if unit == T:
                            act.wait_ge(prep_dve, 1)
                        XT_hi(unit) if unit < T else Q_hi(unit - T)
                        for n in fills_behind(unit):
                            fill_out(n)
                            if PREP[n] == ("K", None, 1):
                                K_copy(0)
                            if PREP[n] == ("K", None, 3):
                                K_copy(1)
                    return
                if isinstance(s, int) and s == 1:
                    late_hi(0), late_hi(1), late_hi(2), late_hi(3), XT_hi(0), late_hi(4), late_hi(5)
                    late_hi(6), late_hi(7), exponent(1), XT_hi(1), XT_hi(2), exponent(2), XT_hi(3)
                    late_hi(12), late_hi(13), Q_hi(0), Q_hi(1), late_hi(14), exponent(3), Q_hi(2), late_hi(15)
                    PT_out(3, 0), Q_hi(3), PT_out(3, 1), PT_out(3, 2), PT_out(3, 3)
                    return
                if isinstance(s, int) and s == 2:
                    XT_hi(0), PT_out(0, 0), XT_hi(1), PT_out(0, 1), XT_hi(2), XT_hi(3), PT_out(0, 2)
                    exponent(0), PT_out(0, 3), exponent(1), PT_out(1, 0), PT_out(1, 1), PT_out(1, 2)
                    exponent(2), PT_out(1, 3), Q_hi(0), Q_hi(1), PT_out(2, 0), Q_hi(2), PT_out(2, 1), V_copy()
                    PT_out(2, 2), PT_out(2, 3), exponent(3), Q_hi(3), PT_out(3, 0), AV_hi(0), AV_hi(1)
                    PT_out(3, 1), PT_out(3, 2), AV_hi(2), AV_hi(3), PT_out(3, 3)
                    return
                if isinstance(s, int) and s == NB:
                    PT_out(0, 0), exponent(0), PT_out(0, 1), PT_out(0, 2), PT_out(0, 3), exponent(1)
                    PT_out(1, 0), PT_out(1, 1), PT_out(1, 2), PT_out(1, 3), exponent(2), PT_out(2, 0)
                    PT_out(2, 1), LN_scale(0), PT_out(2, 2), LN_scale(1), PT_out(2, 3), exponent(3)
                    PT_out(3, 0), AV_hi(0), PT_out(3, 1), AV_hi(1), PT_out(3, 2), AV_hi(2), AV_hi(3)
                    PT_out(3, 3), LN_scale(2), LN_scale(3)
                    return
                if isinstance(s, int) and s == NB + 1:
                    PT_out(0, 0), PT_out(0, 1), PT_out(0, 2), exponent(0), PT_out(0, 3), PT_out(1, 0)
                    PT_out(1, 1), PT_out(1, 2), PT_out(1, 3), PT_out(2, 0), PT_out(2, 1), PT_out(2, 2)
                    PT_out(2, 3), LN_scale(0), AV_hi(0), AV_hi(1), LN_scale(1), AV_hi(2), AV_hi(3)
                    LN_scale(2), LN_scale(3)
                    return
                if isinstance(s, int) and s == NB + 2:
                    LN_scale(0), LN_scale(1), LN_scale(2)
                    return
                exponent(0), PT_out(0, 0), PT_out(0, 1), exponent(1), PT_out(0, 2), PT_out(0, 3), PT_out(1, 0)
                PT_out(1, 1), XT_hi(0), XT_hi(1), PT_out(1, 2), LN_scale(0), XT_hi(2), XT_hi(3), PT_out(1, 3)
                V_copy(), exponent(2), PT_out(2, 0), PT_out(2, 1), K_copy(0), LN_scale(1), PT_out(2, 2)
                Q_hi(0), Q_hi(1), exponent(3), PT_out(2, 3), Q_hi(2), K_copy(1), Q_hi(3), PT_out(3, 0)
                AV_hi(0), AV_hi(1), PT_out(3, 1), LN_scale(2), PT_out(3, 2), AV_hi(2), AV_hi(3), PT_out(3, 3)
                LN_scale(3)

            step(0, 0)
            steps(act, step)

        @block.vector
        def _(dve):
            tt = nc.vector.tensor_tensor

            for i in range(T):
                dve.sem_inc(stored[i], 16)
            for kd in (Kd_hi, Kd_lo):
                nc.vector.memset(kd[:, :, :, :].bitcast(FP32), 0.0).then_inc(Kd_zeroed, 1)

            def fill_out(n):
                kind, w, c = PREP[n]
                if "dve" not in readers(PREP[n]):
                    return
                bank = prep_bank(n)
                dve.wait_ge(prep_ps, n + 1)
                if kind == "bias":
                    last = nc.vector.tensor_copy(qk_bias[:, :], bank[:, 0:2 * C])
                elif kind == "ctxT":
                    dve.wait_ge(prep_act, prep_count("act", n + 1))
                    last = tt(ctxT_lo[:, c, :], bank[:, 0:B * SK], ctxT_hi[:, c, :].bitcast(FP32), ALU.subtract)
                elif kind == "K":
                    dve.wait_ge(prep_act, prep_count("act", n + 1))
                    last = nc.vector.scalar_tensor_tensor(
                        out=K_lo[:, c, :, :].rearrange("p b k -> p (b k)"), in0=bank[:, 0:B * SK],
                        scalar=qk_bias[:, C + c:C + c + 1],
                        in1=K_hi[:, c, :, :].rearrange("p b k -> p (b k)").bitcast(FP32),
                        op0=ALU.add, op1=ALU.subtract)
                elif kind == "V":
                    dve.wait_ge(bv_loaded, 16)
                    last = tt(V_all[:, c, :], bank[0:SK, :], bv_row, ALU.add)
                else:
                    dve.wait_ge(prep_act, prep_count("act", n + 1))
                    cols = slice(c * P, c * P + P)
                    last = tt(W_lo[w][:, :, cols], bank.rearrange("p (k r) -> p k r", k=C),
                              W_hi[w][:, :, cols].bitcast(FP32), ALU.subtract)
                last.then_inc(prep_dve, 1)

            def masks():
                dve.wait_ge(mask_loaded, 16)
                nc.vector.tensor_copy(mask_f[:, :, :], mask_i).then_inc(mask_ready, 1)
                dve.wait_ge(mask_ready, 1)
                nc.vector.tensor_scalar(mask_bias[:, :, :], mask_f[:, :, :], 0.0, NEG,
                                        ALU.is_equal, ALU.mult).then_inc(mask_ready, 1)

            def step(s, phase):
                bx, bs, ba, bo_ = s, s - 1, s - 2, s - 3

                def XT_lo(i):
                    if not has(bx):
                        return
                    dve.wait_ge(xt_hi, 4 * bx + i + 1)
                    cols = slice(i * P, i * P + P)
                    tt(xT_lo[:, :, cols], xt_bank(i).rearrange("p (k r) -> p k r", k=C),
                       xT_hi[:, :, cols].bitcast(FP32), ALU.subtract).then_inc(xt_lo, 1)

                def Q_lo(g):
                    if not has(bx):
                        return
                    dve.wait_ge(q_hi, 4 * bx + g + 1)
                    nc.vector.scalar_tensor_tensor(out=QT_lo[:, phase % 2, g, :], in0=q_bank(g),
                                                   scalar=qk_bias[:, g:g + 1],
                                                   in1=QT_hi[:, phase % 2, g, :].bitcast(FP32),
                                                   op0=ALU.add, op1=ALU.subtract).then_inc(q_ready, 1)

                def bias(t, half):
                    tile = 4 * bs + t
                    if not valid(tile):
                        return
                    dve.wait_ge(s_ps, 2 * tile + half + 1)
                    if half == 0 and (not isinstance(tile, int) or tile >= 4):
                        dve.wait_ge(pt_ps, 4 * tile - 12)
                    tt(E[:, t, 2 * HG * half:2 * HG * half + 2 * HG, :].rearrange("p (g j) k -> p g j k", g=2),
                       scores_ps[:, 2 * half:2 * half + 2, 0:GK].rearrange("p g (j k) -> p g j k", j=HG),
                       mask_bias[:, bass.ds(bs % BB * T + t, 1), :].unsqueeze(2).broadcast_to((P, 2, HG, SK)),
                       ALU.add).then_inc(biased, 1)

                def row_max(t):
                    tile = 4 * bs + t
                    if not valid(tile):
                        return
                    dve.wait_ge(biased, 2 * tile + 2)
                    nc.vector.tensor_reduce(out=rowmax[:, t, :], in_=E[:, t, :, :], op=ALU.max, axis=AX.X) \
                        .then_inc(max_ready, 1)

                def shift(t):
                    tile = 4 * bs + t
                    if not valid(tile):
                        return
                    dve.wait_ge(max_ready, tile + 1)
                    nc.vector.tensor_scalar(exp_bias[:, t, :], rowmax[:, t, HV:H], -1.0 / SCALE, None, ALU.mult) \
                        .then_inc(exp_bias_ready, 1)
                    e = E[:, t, 0:HV, :]
                    tt(e, e, rowmax[:, t, 0:HV].unsqueeze(2).broadcast_to((P, HV, SK)), ALU.subtract) \
                        .then_inc(shifted, 1)

                def row_sum(t):
                    tile = 4 * bs + t - 2
                    if not valid(tile):
                        return
                    i = (t + 2) % 4
                    dve.wait_ge(weighted, tile + 1)
                    nc.vector.tensor_reduce(out=rowsum[:, i, :], in_=E[:, i, :, :], op=ALU.add, axis=AX.X) \
                        .then_inc(sum_ready, 1)

                def sum_eps(t):
                    tile = 4 * bs + t - 2
                    if not valid(tile):
                        return
                    i = (t + 2) % 4
                    dve.wait_ge(sum_ready, tile + 1)
                    nc.vector.tensor_scalar(rowsum_eps[:, i, :], rowsum[:, i, :], SUM_EPS, None, ALU.add) \
                        .then_inc(sum_eps_ready, 1)

                def inverse(t):
                    tile = 4 * bs + t - 2
                    if not valid(tile):
                        return
                    i = (t + 2) % 4
                    dve.wait_ge(sum_eps_ready, tile + 1)
                    nc.vector.reciprocal(inv_sum[:, i, :], rowsum_eps[:, i, :]).then_inc(inv_ready, 1)

                def AV_lo(g):
                    if not has(ba):
                        return
                    dve.wait_ge(at_hi, 4 * ba + g + 1)
                    tt(AT_lo[:, g, :], av_bank(g)[:, :], AT_hi[:, g, :].bitcast(FP32), ALU.subtract) \
                        .then_inc(at_lo, 1)

                def residual(i):
                    if not has(bo_):
                        return
                    tile = 4 * bo_ + i
                    dve.wait_ge(out_ps, tile + 1)
                    dve.wait_ge(x_bo_ready, tile + 1)
                    dve.wait_ge(stored[i], 16 + 16 * bo_)
                    tt(Y[:, i, :], out_bank(i),
                       x_bo[:, bass.ds(bo_ % RING, 1), i, :].rearrange("p r d -> p (r d)"), ALU.add) \
                        .then_inc(y_ready, 1)

                def stats(i):
                    if not has(bo_):
                        return
                    dve.wait_ge(y_ready, 4 * bo_ + i + 1)
                    nc.vector.bn_stats(bn[:, i, :], Y[:, i, :]).then_inc(bn_ready, 1)

                def aggregate(i):
                    if not has(bo_):
                        return
                    dve.wait_ge(bn_ready, 4 * bo_ + i + 1)
                    dve.sem_inc(aggr_turn, 1)
                    nc.vector.bn_aggr(mean_var[:, i, :], bn[:, i, :]).then_inc(stats_ready, 1)

                def center(i):
                    if not has(bo_):
                        return
                    dve.wait_ge(stats_ready, 4 * bo_ + i + 1)
                    nc.vector.scalar_tensor_tensor(out=Y[:, i, :], in0=Y[:, i, :], scalar=mean_var[:, i, 0:1],
                                                   in1=g_row[:, :], op0=ALU.subtract, op1=ALU.mult) \
                        .then_inc(centered, 1)

                def finish(i):
                    tile = 4 * bo_ + i
                    dve.wait_ge(centered, tile + 1)
                    dve.wait_ge(rstd_ready, tile + 1)
                    nc.vector.scalar_tensor_tensor(out=Y[:, i, :], in0=Y[:, i, :], scalar=rstd[:, i:i + 1],
                                                   in1=b_row[:, :], op0=ALU.mult, op1=ALU.add) \
                        .then_inc(finished, 1)

                def late_lo(n):
                    fill_out(EARLY + n)

                if isinstance(s, int) and s == 0:
                    for unit in range(2 * T):
                        XT_lo(unit) if unit < T else Q_lo(unit - T)
                        if unit == 2 * T - 2:
                            masks()
                        for n in fills_behind(unit):
                            fill_out(n)
                    dve.wait_ge(mask_ready, 2)
                    return
                if isinstance(s, int) and s == 1:
                    late_lo(0), late_lo(1), bias(0, 0), late_lo(2), bias(0, 1), late_lo(3), bias(1, 0)
                    row_max(0), bias(1, 1), shift(0), row_max(1), shift(1), XT_lo(0), late_lo(8), bias(2, 0)
                    late_lo(9), XT_lo(1), late_lo(10), XT_lo(2), late_lo(11), XT_lo(3), row_sum(2)
                    late_lo(12), bias(2, 1), row_max(2), late_lo(13), sum_eps(2), inverse(2), Q_lo(0)
                    shift(2), Q_lo(1), late_lo(14), row_sum(3), bias(3, 0), late_lo(15), Q_lo(2), sum_eps(3)
                    inverse(3), bias(3, 1), Q_lo(3), row_max(3), shift(3)
                    return
                if isinstance(s, int) and s == 2:
                    dve.wait_ge(rows_loaded, 32)
                    row_sum(0), XT_lo(0), bias(0, 0), sum_eps(0), bias(0, 1), inverse(0), XT_lo(1), XT_lo(2)
                    XT_lo(3), row_max(0), shift(0), bias(1, 0), bias(1, 1), row_max(1), row_sum(1), shift(1)
                    sum_eps(1), inverse(1), row_sum(2), bias(2, 0), bias(2, 1), row_max(2), sum_eps(2)
                    inverse(2), Q_lo(0), Q_lo(1), shift(2), row_sum(3), Q_lo(2), bias(3, 0), bias(3, 1)
                    Q_lo(3), row_max(3), AV_lo(0), sum_eps(3), inverse(3), AV_lo(1), shift(3), AV_lo(2)
                    AV_lo(3)
                    return
                if isinstance(s, int) and s == NB:
                    row_sum(0), bias(0, 0), bias(0, 1), sum_eps(0), row_max(0), inverse(0), residual(0)
                    shift(0), bias(1, 0), row_sum(1), stats(0), residual(1), sum_eps(1), stats(1), bias(1, 1)
                    aggregate(0), row_max(1), row_sum(2), aggregate(1), sum_eps(2), inverse(1), shift(1)
                    center(0), residual(2), inverse(2), bias(2, 0), center(1), residual(3), stats(2)
                    bias(2, 1), row_max(2), aggregate(2), shift(2), row_sum(3), stats(3), sum_eps(3)
                    center(2), inverse(3), aggregate(3), bias(3, 0), AV_lo(0), center(3), bias(3, 1), AV_lo(1)
                    AV_lo(2), AV_lo(3), row_max(3), shift(3)
                    return
                if isinstance(s, int) and s == NB + 1:
                    row_sum(0), residual(0), stats(0), residual(1), sum_eps(0), aggregate(0), inverse(0)
                    center(0), stats(1), row_sum(1), sum_eps(1), inverse(1), aggregate(1), residual(2)
                    center(1), stats(2), aggregate(2), center(2), residual(3), AV_lo(0), AV_lo(1), AV_lo(2)
                    AV_lo(3), stats(3), aggregate(3), center(3)
                    return
                if isinstance(s, int) and s == NB + 2:
                    residual(0), stats(0), aggregate(0), center(0), residual(1), stats(1), aggregate(1)
                    center(1), residual(2), stats(2), aggregate(2), center(2), residual(3), stats(3)
                    aggregate(3), center(3), finish(3)
                    return
                bias(0, 0), bias(0, 1), row_max(0), shift(0), residual(0), row_sum(0), sum_eps(0), inverse(0)
                row_sum(1), stats(0), residual(1), aggregate(0), sum_eps(1), bias(1, 0), inverse(1)
                bias(1, 1), center(0), stats(1), row_max(1), residual(2), residual(3), aggregate(1), shift(1)
                XT_lo(0), XT_lo(1), bias(2, 0), XT_lo(2), XT_lo(3), stats(2), center(1), bias(2, 1)
                row_sum(2), sum_eps(2), inverse(2), stats(3), row_max(2), shift(2), row_sum(3), aggregate(2)
                Q_lo(0), sum_eps(3), Q_lo(1), aggregate(3), center(2), bias(3, 0), inverse(3), bias(3, 1)
                center(3), Q_lo(2), Q_lo(3), row_max(3), AV_lo(0), AV_lo(1), shift(3), AV_lo(2), AV_lo(3)

            step(0, 0)
            steps(dve, step)

        @block.gpsimd
        def _(pool):
            nc.gpsimd.memset(ident[:, :], 0.0).then_inc(ident_zeroed, 1)
            nc.gpsimd.memset(minus_half[:, :], -0.5).then_inc(ident_zeroed, 1)
            nc.gpsimd.memset(ln_eps[:, :], LN_EPS).then_inc(ident_zeroed, 1)
            pool.wait_ge(ident_zeroed, 3)
            nc.gpsimd.affine_select(out=ident[:, :], in_=ident[:, :], compare_op=ALU.not_equal, fill=1.0,
                                    base=0, pattern=[[-1, P]], channel_multiplier=1).then_inc(ident_ready, 1)
            pool.wait_ge(bo_loaded, 16)

            def step(s, phase):
                bx, bs, bo_ = s, s - 1, s - 3

                def add_bo(i):
                    if not has(bx):
                        return
                    pool.wait_ge(x_loaded[i], 16 * bx + 16)
                    if not isinstance(bx, int) or bx >= RING:
                        pool.wait_ge(y_ready, 4 * (bx - RING) + i + 1)
                    nc.gpsimd.tensor_tensor(out=x_bo[:, bass.ds(bx % RING, 1), i, :].rearrange("p r d -> p (r d)"),
                                            in0=x_in[:, i, :], in1=bo_row[:, :], op=ALU.add) \
                        .then_inc(x_bo_ready, 1)

                def weigh(t):
                    tile = 4 * bs + t - 1
                    if not valid(tile):
                        return
                    pool.wait_ge(exp_ready, tile + 1)
                    e = E[:, (t + 3) % 4, :, :]
                    b_tile = (bs * T + t - 1) % MT
                    nc.gpsimd.tensor_tensor(out=e, in0=e, in1=mask_f[:, bass.ds(b_tile, 1), :]
                                            .broadcast_to((P, H, SK)), op=ALU.mult).then_inc(weighted, 1)

                def normalise(t):
                    tile = 4 * bs + t - 2
                    if not valid(tile):
                        return
                    i = (t + 2) % 4
                    pool.wait_ge(inv_ready, tile + 1)
                    e = E[:, i, :, :]
                    nc.gpsimd.tensor_tensor(out=e, in0=e, in1=inv_sum[:, i, :].unsqueeze(2)
                                            .broadcast_to((P, H, SK)), op=ALU.mult).then_inc(probs_ready, 1)

                def inv_std(i):
                    if not has(bo_):
                        return
                    tile = 4 * bo_ + i
                    pool.wait_ge(stats_ready, tile + 1)
                    nc.gpsimd.tensor_tensor(out=var_eps[:, i:i + 1], in0=mean_var[:, i, 1:2], in1=ln_eps[:, :],
                                            op=ALU.add).then_inc(var_eps_ready, 1)
                    pool.wait_ge(var_eps_ready, tile + 1)
                    nc.gpsimd.tensor_tensor(out=rstd[:, i:i + 1], in0=var_eps[:, i:i + 1],
                                            in1=minus_half[:, :], op=ALU.pow).then_inc(rstd_ready, 1)

                def add_beta(i):
                    if not has(bo_):
                        return
                    pool.wait_ge(scaled, 4 * bo_ + i + 1)
                    nc.gpsimd.tensor_tensor(out=Y[:, i, :], in0=Y[:, i, :], in1=b_row[:, :], op=ALU.add) \
                        .then_inc(normed, 1)

                if isinstance(s, int) and s == 0:
                    add_bo(0), add_bo(1), add_bo(2), add_bo(3)
                    return
                if isinstance(s, int) and s == 1:
                    pool.wait_ge(mask_ready, 2)
                    weigh(1), add_bo(0), add_bo(1), weigh(2), add_bo(2), normalise(2), add_bo(3), weigh(3)
                    normalise(3)
                    return
                if isinstance(s, int) and s == 2:
                    pool.wait_ge(prep_ps, PREP.index(("VT", None, C - 1)) + 1)
                    pool.wait_ge(rows_loaded, 32)
                    normalise(0), add_bo(0), weigh(0), add_bo(1), weigh(1), normalise(1), weigh(2), add_bo(2)
                    normalise(2), weigh(3), add_bo(3), normalise(3)
                    return
                if isinstance(s, int) and s == NB:
                    weigh(0), normalise(0), weigh(1), normalise(1), inv_std(0), inv_std(1), weigh(2)
                    normalise(2), add_beta(0), inv_std(2), normalise(3), inv_std(3), add_beta(1), weigh(3)
                    add_beta(2), add_beta(3)
                    return
                if isinstance(s, int) and s == NB + 1:
                    weigh(0), normalise(0), normalise(1), inv_std(0), inv_std(1), add_beta(0), add_beta(1)
                    inv_std(2), inv_std(3), add_beta(2), add_beta(3)
                    return
                if isinstance(s, int) and s == NB + 2:
                    inv_std(0), inv_std(1), add_beta(0), inv_std(2), add_beta(1), inv_std(3), add_beta(2)
                    return
                weigh(0), normalise(0), inv_std(0), normalise(1), add_bo(0), add_bo(1), weigh(1), weigh(2)
                inv_std(1), normalise(2), add_bo(2), add_beta(0), inv_std(2), normalise(3), weigh(3)
                add_beta(1), inv_std(3), add_bo(3), add_beta(2), add_beta(3)

            step(0, 0)
            steps(pool, step)


_INPUTS = ["x", "ctx_1024", "mask_1x1xSxS2_if1", "L0_xattn_Wq", "L0_xattn_bq", "L0_xattn_Wk", "L0_xattn_bk",
           "L0_xattn_Wv", "L0_xattn_bv", "L0_xattn_Wo", "L0_xattn_bo", "L0_xattn_ln_g", "L0_xattn_ln_b"]


def kernel(**inputs):
    import concourse.bacc as bacc
    from concourse.bass_utils import run_bass_kernel_spmd

    nc = bacc.Bacc("TRN2", target_bir_lowering=False, num_devices=1, dynamic_dma_scratch_size=1024)
    arrays, args = {}, []
    for name in _INPUTS:
        a = np.ascontiguousarray(inputs[name])
        arrays[f"in_{name}"] = a
        args.append(nc.dram_tensor(f"in_{name}", a.shape, mybir.dt.from_np(a.dtype), kind="ExternalInput").ap())
    out = nc.dram_tensor("out_y", inputs["x"].shape, FP32, kind="ExternalOutput").ap()
    xattn_program(nc, *args, out)
    result = run_bass_kernel_spmd(nc, [arrays], core_ids=[0])
    return result.results[0]["out_y"]
```
